# Optimizing a Trainium2 kernel written in Bass

```python
import numpy as np
import jax
import jax.numpy as jnp

def _softmax(x, axis=-1):
    return jax.nn.softmax(x, axis=axis)

def _gelu(x):
    return jax.nn.gelu(x, approximate=True)

def _silu(x):
    return jax.nn.silu(x)

def _sigmoid(x):
    return jax.nn.sigmoid(x)

def _layernorm(x, axis=-1, eps=1e-05):
    m = jnp.mean(x, axis=axis, keepdims=True)
    v = jnp.var(x, axis=axis, keepdims=True)
    return (x - m) / jnp.sqrt(v + eps)

def _scatter_add(tgt, idx, src, axis=0):
    return tgt.at[idx].add(src)

def _segment_sum(src, seg, n):
    return jax.ops.segment_sum(src, seg, n)
kernel_name = 'mk_recurrent_d2_jaxref_r8_fc708a'

def setup_inputs(seed: int=0):
    np.random.seed(seed)
    _w = jnp.asarray

    def _L0_attn_setup():
        import jax, jax.numpy as jnp
        import numpy as np
        key = jax.random.key(seed)
        k1, k2, k3, k4 = jax.random.split(key, 4)
        B, N, D = (4, 256, 128)
        D1, D2 = (128, 128)
        X = jax.random.normal(k1, (B, N, D), dtype=jnp.float32)
        s_q = (2.0 / (D + D1)) ** 0.5
        s_v = (2.0 / (D + D2)) ** 0.5
        W_Q = jax.random.normal(k2, (D, D1), dtype=jnp.float32) * s_q
        W_K = jax.random.normal(k3, (D, D1), dtype=jnp.float32) * s_q
        W_V = jax.random.normal(k4, (D, D2), dtype=jnp.float32) * s_v
        return {'X': X, 'W_Q': W_Q, 'W_K': W_K, 'W_V': W_V}
    _L0_attn_in = _L0_attn_setup()

    def _L0_ffn_setup():
        import jax, jax.numpy as jnp
        import numpy as np
        EMBED = 128
        NUM_EXPERTS = 8
        TOP_K = 2
        key = jax.random.key(seed)
        ks = jax.random.split(key, 6)
        scale = EMBED ** (-0.5)
        return {'x': jax.random.normal(ks[0], (4, 512, EMBED), jnp.float32), 'router_w': jax.random.normal(ks[1], (EMBED, NUM_EXPERTS), jnp.float32) * scale, 'router_b': jnp.zeros((NUM_EXPERTS,), jnp.float32), 'we_gate': jax.random.normal(ks[2], (NUM_EXPERTS, EMBED, EMBED), jnp.float32) * scale, 'we_up': jax.random.normal(ks[3], (NUM_EXPERTS, EMBED, EMBED), jnp.float32) * scale, 'we_down': jax.random.normal(ks[4], (NUM_EXPERTS, EMBED, EMBED), jnp.float32) * scale}
    _L0_ffn_in = _L0_ffn_setup()

    def _L1_attn_setup():
        import jax, jax.numpy as jnp
        import numpy as np
        H = 8
        ROPE_DIM = 64
        GAMMA = 0.96875
        GROUPS = 16
        EPS = 1e-05

        def _rope(x, offset=0):
            T = x.shape[-2]
            inv_freq = 1.0 / 10000.0 ** (np.arange(0, ROPE_DIM, 2, dtype=np.float32) / ROPE_DIM)
            t = jnp.arange(T, dtype=jnp.float32) + offset
            freqs = t[:, None] * inv_freq[None, :]
            freqs = jnp.repeat(freqs, 2, axis=-1)
            cos, sin = (jnp.cos(freqs), jnp.sin(freqs))
            xr, xp = (x[..., :ROPE_DIM], x[..., ROPE_DIM:])
            x1, x2 = (xr[..., 0::2], xr[..., 1::2])
            rot = jnp.stack([-x2, x1], axis=-1).reshape(xr.shape)
            return jnp.concatenate([xr * cos + rot * sin, xp], axis=-1)

        def _to_scores(X, W):
            B, T, C = X.shape
            return (X @ W).reshape(B, T, H, C).transpose(0, 2, 1, 3)
        key = jax.random.key(seed)
        ks = jax.random.split(key, 4)
        B, T, C = (1, 256, 128)
        return {'X_Q': jax.random.normal(ks[0], (B, T, C), jnp.float32), 'W_Q': jax.random.normal(ks[1], (C, C * H), jnp.float32) / C, 'W_K': jax.random.normal(ks[2], (C, C * H), jnp.float32) / C, 'W_V': jax.random.normal(ks[3], (C, C * H), jnp.float32) / C, 'gn_weight': jnp.ones((C,), jnp.float32), 'gn_bias': jnp.zeros((C,), jnp.float32)}
    _L1_attn_in = _L1_attn_setup()

    def _L1_ffn_setup():
        import jax, jax.numpy as jnp
        import numpy as np
        TOP_K = 4
        CAP_FACTOR = 4

        def swiglu(x, w1, w2, w3):
            return jax.nn.silu(x @ w1) * (x @ w3) @ w2
        key = jax.random.key(seed)
        ks = jax.random.split(key, 8)
        B, S, D, H, E = (2, 256, 128, 64, 32)
        Hs = 2 * H
        sd = lambda *sh: 1.0 / np.sqrt(sh[-2])
        x = jax.random.normal(ks[0], (B, S, D), dtype=jnp.float32)
        Wg = jax.random.normal(ks[1], (D, E), dtype=jnp.float32) * (1.0 / np.sqrt(D))
        W1 = jax.random.normal(ks[2], (E, D, H), dtype=jnp.float32) * (1.0 / np.sqrt(D))
        W3 = jax.random.normal(ks[3], (E, D, H), dtype=jnp.float32) * (1.0 / np.sqrt(D))
        W2 = jax.random.normal(ks[4], (E, H, D), dtype=jnp.float32) * (1.0 / np.sqrt(H))
        Ws1 = jax.random.normal(ks[5], (D, Hs), dtype=jnp.float32) * (1.0 / np.sqrt(D))
        Ws3 = jax.random.normal(ks[6], (D, Hs), dtype=jnp.float32) * (1.0 / np.sqrt(D))
        Ws2 = jax.random.normal(ks[7], (Hs, D), dtype=jnp.float32) * (1.0 / np.sqrt(Hs))
        return {'x': x, 'Wg': Wg, 'W1': W1, 'W2': W2, 'W3': W3, 'Ws1': Ws1, 'Ws2': Ws2, 'Ws3': Ws3}
    _L1_ffn_in = _L1_ffn_setup()
    _d = {'L0_attn_X': _L0_attn_in['X'], 'L0_attn_W_Q': _L0_attn_in['W_Q'], 'L0_attn_W_K': _L0_attn_in['W_K'], 'L0_attn_W_V': _L0_attn_in['W_V'], 'L0_ffn_router_w': _L0_ffn_in['router_w'], 'L0_ffn_router_b': _L0_ffn_in['router_b'], 'L0_ffn_we_gate': _L0_ffn_in['we_gate'], 'L0_ffn_we_up': _L0_ffn_in['we_up'], 'L0_ffn_we_down': _L0_ffn_in['we_down'], 'L1_attn_W_Q': _L1_attn_in['W_Q'], 'L1_attn_W_K': _L1_attn_in['W_K'], 'L1_attn_W_V': _L1_attn_in['W_V'], 'L1_attn_gn_weight': _L1_attn_in['gn_weight'], 'L1_attn_gn_bias': _L1_attn_in['gn_bias'], 'L1_ffn_Wg': _L1_ffn_in['Wg'], 'L1_ffn_W1': _L1_ffn_in['W1'], 'L1_ffn_W2': _L1_ffn_in['W2'], 'L1_ffn_W3': _L1_ffn_in['W3'], 'L1_ffn_Ws1': _L1_ffn_in['Ws1'], 'L1_ffn_Ws2': _L1_ffn_in['Ws2'], 'L1_ffn_Ws3': _L1_ffn_in['Ws3']}
    _x0 = _d['L0_attn_X']
    _d['L0_attn_X'] = jax.random.normal(jax.random.fold_in(jax.random.key(seed), 1), (8, 1024, 128), dtype=_x0.dtype)
    del _x0
    return _d

def reference(L0_attn_X, L0_attn_W_Q, L0_attn_W_K, L0_attn_W_V, L0_ffn_router_w, L0_ffn_router_b, L0_ffn_we_gate, L0_ffn_we_up, L0_ffn_we_down, L1_attn_W_Q, L1_attn_W_K, L1_attn_W_V, L1_attn_gn_weight, L1_attn_gn_bias, L1_ffn_Wg, L1_ffn_W1, L1_ffn_W2, L1_ffn_W3, L1_ffn_Ws1, L1_ffn_Ws2, L1_ffn_Ws3):

    def _L0_attn_ref(X, W_Q, W_K, W_V):
        import jax, jax.numpy as jnp
        import numpy as np
        D1 = W_Q.shape[1]
        Q = jnp.einsum('bnd,de->bne', X, W_Q)
        K = jnp.einsum('bnd,de->bne', X, W_K)
        V = jnp.einsum('bnd,de->bne', X, W_V)
        scale = 1.0 / jnp.sqrt(jnp.asarray(D1, dtype=X.dtype))
        A = jnp.einsum('bne,bme->bnm', Q, K) * scale
        A = jax.nn.softmax(A, axis=-1)
        return jnp.einsum('bnm,bme->bne', A, V)

    def _L0_ffn_ref(x, router_w, router_b, we_gate, we_up, we_down):
        import jax, jax.numpy as jnp
        import numpy as np
        EMBED = 128
        NUM_EXPERTS = 8
        TOP_K = 2
        x_shape = x.shape
        x_flat = x.reshape(-1, x_shape[-1])
        num_tokens = x_flat.shape[0]
        router_logits = x_flat @ router_w + router_b
        topk_weights, topk_indices = jax.lax.top_k(router_logits, k=TOP_K)
        topk_weights = jax.nn.softmax(topk_weights, axis=-1)
        token_idx_mesh = jnp.repeat(jnp.arange(num_tokens), TOP_K)
        expert_idx_mesh = topk_indices.reshape(-1)
        sort_permutation = jnp.argsort(expert_idx_mesh)
        sorted_expert_idx = expert_idx_mesh[sort_permutation]
        sorted_token_idx = token_idx_mesh[sort_permutation]
        group_sizes = jnp.bincount(sorted_expert_idx, length=NUM_EXPERTS)
        sorted_tokens = x_flat[sorted_token_idx]
        ff_gate = jax.lax.ragged_dot(sorted_tokens, we_gate, group_sizes)
        ff_up = jax.lax.ragged_dot(sorted_tokens, we_up, group_sizes)
        activated = jax.nn.silu(ff_gate) * ff_up
        ff_out = jax.lax.ragged_dot(activated, we_down, group_sizes)
        sorted_weights = topk_weights.reshape(-1)[sort_permutation]
        ff_out = ff_out * sorted_weights[:, None]
        output_flat = jnp.zeros_like(x_flat).at[sorted_token_idx].add(ff_out)
        return output_flat.reshape(x_shape)

    def _L1_attn_ref(X_Q, W_Q, W_K, W_V, gn_weight, gn_bias):
        import jax, jax.numpy as jnp
        import numpy as np
        H = 8
        ROPE_DIM = 64
        GAMMA = 0.96875
        GROUPS = 16
        EPS = 1e-05

        def _rope(x, offset=0):
            T = x.shape[-2]
            inv_freq = 1.0 / 10000.0 ** (np.arange(0, ROPE_DIM, 2, dtype=np.float32) / ROPE_DIM)
            t = jnp.arange(T, dtype=jnp.float32) + offset
            freqs = t[:, None] * inv_freq[None, :]
            freqs = jnp.repeat(freqs, 2, axis=-1)
            cos, sin = (jnp.cos(freqs), jnp.sin(freqs))
            xr, xp = (x[..., :ROPE_DIM], x[..., ROPE_DIM:])
            x1, x2 = (xr[..., 0::2], xr[..., 1::2])
            rot = jnp.stack([-x2, x1], axis=-1).reshape(xr.shape)
            return jnp.concatenate([xr * cos + rot * sin, xp], axis=-1)

        def _to_scores(X, W):
            B, T, C = X.shape
            return (X @ W).reshape(B, T, H, C).transpose(0, 2, 1, 3)
        B, T, C = X_Q.shape
        Q = _rope(_to_scores(X_Q, W_Q))
        K = _rope(_to_scores(X_Q, W_K))
        V = _to_scores(X_Q, W_V)
        Q, K, V = (jax.nn.silu(Q), jax.nn.silu(K), jax.nn.silu(V))
        n = jnp.arange(T)
        diff = n[:, None] - n[None, :]
        D = jnp.where(diff >= 0, GAMMA ** jnp.maximum(diff, 0).astype(jnp.float32), 0.0)
        A = jnp.einsum('bhqc,bhkc->bhqk', Q, K)
        A = A * D
        A = jnp.swapaxes(A, -2, -1)
        out = A @ V
        out = out.sum(axis=1)
        x = out.reshape(B * T, GROUPS, C // GROUPS)
        mu = x.mean(-1, keepdims=True)
        var = x.var(-1, keepdims=True)
        xn = (x - mu) * jax.lax.rsqrt(var + EPS)
        out = xn.reshape(B * T, C) * gn_weight + gn_bias
        return out.reshape(B, T, C)

    def _L1_ffn_ref(x, Wg, W1, W2, W3, Ws1, Ws2, Ws3):
        import jax, jax.numpy as jnp
        import numpy as np
        TOP_K = 4
        CAP_FACTOR = 4

        def swiglu(x, w1, w2, w3):
            return jax.nn.silu(x @ w1) * (x @ w3) @ w2
        B, S, D = x.shape
        E = Wg.shape[1]
        T = B * S
        xf = x.reshape(T, D)
        scores = jax.nn.softmax(xf @ Wg, axis=-1)
        weights, indices = jax.lax.top_k(scores, TOP_K)
        P = T * TOP_K
        pair_expert = indices.reshape(-1)
        pair_token = jnp.repeat(jnp.arange(T), TOP_K)
        pair_weight = weights.reshape(-1).astype(xf.dtype)
        C = CAP_FACTOR * P // E
        y = jnp.zeros_like(xf)
        for e in range(E):
            pos = jnp.nonzero(pair_expert == e, size=C, fill_value=P)[0]
            valid = pos < P
            safe = jnp.minimum(pos, P - 1)
            tok = jnp.where(valid, pair_token[safe], 0)
            w = jnp.where(valid, pair_weight[safe], 0.0)
            xg = xf[tok]
            out = swiglu(xg, W1[e], W2[e], W3[e]) * w[:, None]
            y = y.at[tok].add(out)
        z = swiglu(xf, Ws1, Ws2, Ws3)
        return (y + z).reshape(B, S, D)
    x = L0_attn_X
    xn = _layernorm(x, axis=-1)
    s = _L0_attn_ref(xn, L0_attn_W_Q, L0_attn_W_K, L0_attn_W_V)
    g = _silu(_L0_ffn_ref(xn, L0_ffn_router_w, L0_ffn_router_b, L0_ffn_we_gate, L0_ffn_we_up, L0_ffn_we_down))
    x = x + s * g
    xn = _layernorm(x, axis=-1)
    s = _L1_attn_ref(xn, L1_attn_W_Q, L1_attn_W_K, L1_attn_W_V, L1_attn_gn_weight, L1_attn_gn_bias)
    g = _silu(_L1_ffn_ref(xn, L1_ffn_Wg, L1_ffn_W1, L1_ffn_W2, L1_ffn_W3, L1_ffn_Ws1, L1_ffn_Ws2, L1_ffn_Ws3))
    x = x + s * g
    return x

_drawn_inputs = setup_inputs


def setup_inputs(seed=0):
    import zlib

    import numpy as np

    out = dict(_drawn_inputs(seed))
    spreads = {'L0_ffn_router_b': (0.0, 0.1),
     'L1_attn_gn_weight': (1.0, 0.2),
     'L1_attn_gn_bias': (0.0, 0.1)}
    factors = {}
    for name, (base, spread) in spreads.items():
        noise = np.random.default_rng([zlib.crc32(name.encode()), seed]).standard_normal(out[name].shape)
        drawn = base * np.exp(spread * noise) if base else spread * noise
        out[name] = jnp.asarray(drawn.astype(out[name].dtype))
    for name, factor in factors.items():
        out[name] = (out[name] * factor).astype(out[name].dtype)
    return out
```

```python
import numpy as np
import concourse.bass as bass
from concourse import mybir
from contextlib import ExitStack

F32 = mybir.dt.float32
BF16 = mybir.dt.bfloat16
U32 = mybir.dt.uint32
ALU = mybir.AluOpType
ACT = mybir.ActivationFunctionType
AX = mybir.AxisListType

P = 128
B, T, D = 8, 1024, 128
NT = T // P
HALF = NT // 2
BANK = 512
EPS = 1e-5
E0, F0, K0 = 8, 128, 2
E1, F1, K1 = 32, 64, 4
CAP = 4 * (B * T * K1) // E1
H = 8
GAMMA = 0.96875
ROPE = 64
GROUPS = 16
GW = D // GROUPS
GU = 256
HB = BANK // D


def constants():
    pos = np.arange(T, dtype=np.float32)
    inv = (1.0 / 10000.0 ** (np.arange(0, ROPE, 2, dtype=np.float32) / ROPE)).astype(np.float32)
    ang = np.repeat(pos[:, None] * inv[None, :], 2, axis=-1).astype(np.float64)
    cos = np.concatenate([np.cos(ang), np.ones((T, D - ROPE))], axis=1)
    sin = np.sin(ang) * np.where(np.arange(ROPE) % 2 == 0, -1.0, 1.0)
    tiles = lambda a: np.ascontiguousarray(a.reshape(NT, P, -1).transpose(1, 0, 2).astype(np.float32))
    p = np.arange(P)
    grow = GAMMA ** (np.arange(T, dtype=np.float64))
    return {
        "c_ident": np.eye(P, dtype=np.float32),
        "c_cos": tiles(cos),
        "c_sin": tiles(sin),
        "c_causal": (p[:, None] >= p[None, :]).astype(np.float32),
        "c_before": (p[:, None] < p[None, :]).astype(np.float32),
        "c_decay": tiles(grow[:, None])[:, :, 0].copy(),
        "c_undecay": tiles(1.0 / grow[:, None])[:, :, 0].copy(),
        "c_iota": np.tile(np.arange(E1, dtype=np.float32), (P, 1)),
    }


def two_layer_block(nc, a, out):
    ctx = ExitStack()
    with ctx:
        def sb(name, shape, dt=F32):
            return ctx.enter_context(nc.sbuf_tensor(name, shape, dt))

        signals = []

        def signal(name):
            signals.append(ctx.enter_context(nc.semaphore(name)))
            return signals[-1]

        class Chain:

            def __init__(self, signal, eng):
                self.sem, self.eng, self.n = signal, eng, 0

            def link(self, ins):
                self.n += 1
                ins.then_inc(self.sem, 1)
                self.eng.wait_ge(self.sem, self.n)

        ident = sb("ident", [P, P])
        cos = sb("cos", [P, NT, D])
        sin = sb("sin", [P, NT, ROPE])
        causal = sb("causal", [P, P])
        before = sb("before", [P, P])
        before_h = sb("before_h", [P, P], BF16)
        ones_h = sb("ones_h", [P, P], BF16)
        decay = sb("decay", [P, NT])
        undecay = sb("undecay", [P, NT])
        iota = sb("iota", [P, E1])
        wqkv0 = sb("wqkv0", [P, 3, D])
        wr0 = sb("wr0", [P, E0])
        br0 = sb("br0", [P, E0])
        gu0 = sb("gu0", [P, E0 * F0 // GU, 2, GU])
        dn0 = sb("dn0", [P, E0 * F0 // P, D])
        wqkv1 = sb("wqkv1", [P, 3, H * D])
        wr1 = sb("wr1", [P, E1])
        gu1 = sb("gu1", [P, E1 * F1 // GU, 2, GU])
        dn1 = sb("dn1", [P, E1 * F1 // P, D])
        gus = sb("gus", [P, 2, D])
        dns = sb("dns", [P, D])
        gnw = sb("gnw", [P, D])
        gnb = sb("gnb", [P, D])

        x0 = sb("x0", [P, NT, D])
        x1 = sb("x1", [P, NT, D])
        y = sb("y", [P, NT, D])
        xn = sb("xn", [P, NT, D])
        xT = sb("xT", [P, T])
        stats = sb("stats", [P, NT, 6])
        mv = sb("mv", [P, NT, 2])
        std = sb("std", [P, NT])
        rstd = sb("rstd", [P, NT])
        eps = sb("eps", [P, 1])
        lg = sb("lg", [P, NT, E1])
        top = sb("top", [P, NT, 8])
        tix = sb("tix", [P, NT, 8], U32)
        tif = sb("tif", [P, NT, 8])
        hot = sb("hot", [P, NT, E1])
        mask = sb("mask", [P, NT, E1])
        mask_h = sb("mask_h", [P, NT * E1], BF16)
        le = sb("le", [P, NT, E1])
        ex = sb("ex", [P, NT, E1])
        esum = sb("esum", [P, NT])
        rsum = sb("rsum", [P, NT])
        wt = [sb(f"wt{i}", [P, NT, E1]) for i in range(2)]
        running = sb("running", [P, E1])
        qT = sb("qT", [P, T])
        kT = sb("kT", [P, T])
        v0 = sb("v0", [P, NT, D])
        pr = [sb(f"pr{i}", [P, T]) for i in range(2)]
        pT = [sb(f"pT{i}", [P, T]) for i in range(2)]
        mx = sb("mx", [P, NT])
        nmx = sb("nmx", [P, NT])
        den = sb("den", [P, NT])
        rden = sb("rden", [P, NT])
        s0 = sb("s0", [P, NT, D])
        sg = [sb(f"sg{i}", [P, GU]) for i in range(2)]
        hm = [sb(f"hm{i}", [P, GU]) for i in range(2)]
        hw = [sb(f"hw{i}", [P, GU]) for i in range(2)]
        hT = [sb(f"hT{i}", [P, GU]) for i in range(2)]
        gate = sb("gate", [P, 2, BANK])
        gs = sb("gs", [P, 2, BANK])
        rp = sb("rp", [P, 2, H * D])
        rsn = sb("rsn", [P, HB, ROPE])
        rQT = sb("rQT", [P, H * D])
        rKT = sb("rKT", [P, H * D])
        rQ = [sb(f"rQ{i}", [P, H * D]) for i in range(2)]
        rV = [sb(f"rV{i}", [P, H * D]) for i in range(2)]
        rVs = [sb(f"rVs{i}", [P, H * D]) for i in range(2)]
        rA = sb("rA", [P, H * D])
        rS = [sb(f"rS{i}", [P, H * D]) for i in range(2)]
        ret = sb("ret", [P, NT, D])
        gsum = sb("gsum", [P, NT * GROUPS])
        gdev = sb("gdev", [P, NT * D])
        gsq = rA
        gvar = sb("gvar", [P, NT * GROUPS])
        gstd = sb("gstd", [P, NT * GROUPS])
        grs = sb("grs", [P, NT * GROUPS])

        psum = ctx.enter_context(nc.psum_tensor("psum", [P, 8 * BANK], F32))
        bank = [psum[:, i * BANK:(i + 1) * BANK] for i in range(8)]

        s_w = ctx.enter_context(nc.semaphore("s_w"))
        s_const = ctx.enter_context(nc.semaphore("s_const"))
        x_in = ctx.enter_context(nc.semaphore("x_in"))
        y_out = ctx.enter_context(nc.semaphore("y_out"))
        turn_over = ctx.enter_context(nc.semaphore("turn_over"))
        turn_next = ctx.enter_context(nc.semaphore("turn_next"))
        counted = ctx.enter_context(nc.semaphore("counted"))
        dve_done = signal("dve_done")
        y_ready = signal("y_ready")
        ln_var = [signal(f"ln_var{i}") for i in range(2)]
        ln_std = [signal(f"ln_std{i}") for i in range(2)]
        ln_xn = [signal(f"ln_xn{i}") for i in range(2)]
        xT_ps = [signal(f"xT_ps{i}") for i in range(2)]
        xT_sb = [signal(f"xT_sb{i}") for i in range(2)]
        r_lg = [signal(f"r_lg{i}") for i in range(2)]
        r_ev = [signal(f"r_ev{i}") for i in range(2)]
        r_le = [signal(f"r_le{i}") for i in range(2)]
        r_ex = [signal(f"r_ex{i}") for i in range(2)]
        r_mask = signal("r_mask")
        r_rank = signal("r_rank")
        r_rank_read = signal("r_rank_read")
        a_proj = signal("a_proj")
        a_qk = signal("a_qk")
        a_v = signal("a_v")
        a_s = signal("a_s")
        a_nmx = signal("a_nmx")
        a_p = signal("a_p")
        a_pT = signal("a_pT")
        a_pTd = signal("a_pTd")
        a_pTa = signal("a_pTa")
        a_o = signal("a_o")
        a_od = signal("a_od")
        m_gu = [signal(f"m_gu{i}") for i in range(2)]
        m_sg = [signal(f"m_sg{i}") for i in range(2)]
        m_hm = [signal(f"m_hm{i}") for i in range(2)]
        m_hw = [signal(f"m_hw{i}") for i in range(2)]
        m_t = [signal(f"m_t{i}") for i in range(2)]
        m_hT = [signal(f"m_hT{i}") for i in range(2)]
        m_d = [signal(f"m_d{i}") for i in range(2)]
        m_g = [signal(f"m_g{i}") for i in range(2)]
        x1_ready = signal("x1_ready")
        t_proj = signal("t_proj")
        t_rope = signal("t_rope")
        t_v = signal("t_v")
        t_vs = signal("t_vs")
        t_t = signal("t_t")
        t_tT = signal("t_tT")
        t_q = signal("t_q")
        t_a = signal("t_a")
        t_am = signal("t_am")
        t_g = signal("t_g")
        t_gs = signal("t_gs")
        t_o = signal("t_o")
        t_od = signal("t_od")
        g_var = signal("g_var")
        g_std = signal("g_std")
        n_groups = [E0 * F0 // GU, E1 * F1 // GU]

        n_loads = 23 + 2 * sum(n_groups) + 2
        y_store = out.rearrange("b (t p) d -> p (b t) d", p=P)
        x_load = a["L0_attn_X"].rearrange("b (t p) d -> p (b t) d", p=P)
        gu, dn, wr, xs, experts = [gu0, gu1], [dn0, dn1], [wr0, wr1], [x0, x1], [E0, E1]
        W = [F0, F1]
        CHUNK = lambda i: NT - 1 - i

        def end_turn(eng, b):
            eng.drain().then_inc(turn_over, 1)
            eng.wait_ge(turn_next, b + 1)
            eng.sem_inc(counted, 1)

        block = ctx.enter_context(nc.Block())

        def moe_items(layer):
            groups = list(range((E0 * F0 if layer == 0 else E1 * F1) // GU)) + ([None] if layer else [])
            return [(t, g, GU if g is not None else D, g == groups[-1]) for t in range(NT) for g in groups]

        @block.sync
        def _(sp):
            loads = [
                (ident[:], a["c_ident"]), (cos[:], a["c_cos"]), (sin[:], a["c_sin"]), (causal[:], a["c_causal"]),
                (before[:], a["c_before"]), (decay[:], a["c_decay"]), (undecay[:], a["c_undecay"]),
                (iota[:], a["c_iota"]),
                (wqkv0[:, 0, :], a["L0_attn_W_Q"]), (wqkv0[:, 1, :], a["L0_attn_W_K"]), (wqkv0[:, 2, :], a["L0_attn_W_V"]),
                (wr0[:], a["L0_ffn_router_w"]),
                (br0[:], a["L0_ffn_router_b"].rearrange("(o e) -> o e", o=1).to_broadcast([P, E0])),
                (wqkv1[:, 0, :], a["L1_attn_W_Q"]), (wqkv1[:, 1, :], a["L1_attn_W_K"]), (wqkv1[:, 2, :], a["L1_attn_W_V"]),
                (wr1[:], a["L1_ffn_Wg"]),
                (gus[:, 0, :], a["L1_ffn_Ws1"]), (gus[:, 1, :], a["L1_ffn_Ws3"]), (dns[:], a["L1_ffn_Ws2"]),
                (gnw[:], a["L1_attn_gn_weight"].rearrange("(o e) -> o e", o=1).to_broadcast([P, D])),
                (gnb[:], a["L1_attn_gn_bias"].rearrange("(o e) -> o e", o=1).to_broadcast([P, D])),
                (dn0[:], a["L0_ffn_we_down"].rearrange("e f d -> f e d")),
            ]
            for dst, src in loads:
                sp.dma_start(dst, src).then_inc(s_w, 16)
            n = len(loads)
            per0, per1 = GU // F0, GU // F1
            for g in range(E0 * F0 // GU):
                for half, name in enumerate(("L0_ffn_we_gate", "L0_ffn_we_up")):
                    sp.dma_start(gu0[:, g, half, :].rearrange("d (e f) -> d e f", e=per0),
                                 a[name][g * per0:(g + 1) * per0].rearrange("e d f -> d e f")).then_inc(s_w, 16)
                    n += 1
            for g in range(E1 * F1 // GU):
                for half, name in enumerate(("L1_ffn_W1", "L1_ffn_W3")):
                    sp.dma_start(gu1[:, g, half, :].rearrange("d (e f) -> d e f", e=per1),
                                 a[name][g * per1:(g + 1) * per1].rearrange("e d f -> d e f")).then_inc(s_w, 16)
                    n += 1
            w2 = a["L1_ffn_W2"].rearrange("(g e) f d -> e f g d", e=2)
            for e in range(2):
                sp.dma_start(dn1[e * F1:(e + 1) * F1, :, :], w2[e]).then_inc(s_w, 16)
                n += 1
            assert n == n_loads, n

            sp.sem_inc(y_out, 16)
            sp.dma_start(x0[:], x_load[:, 0:NT, :]).then_inc(x_in, 16)
            with sp.Fori(0, B - 1) as b:
                sp.wait_ge(x1_ready, 2)
                sp.dma_start(x0[:], x_load[:, bass.ds(b * NT + NT, NT), :]).then_inc(x_in, 16)
                sp.wait_ge(y_ready, 2)
                sp.dma_start(y_store[:, bass.ds(b * NT, NT), :], y[:]).then_inc(y_out, 16)
                end_turn(sp, b)
            sp.wait_ge(y_ready, 2)
            sp.dma_start(y_store[:, (B - 1) * NT:, :], y[:]).then_inc(y_out, 16)
            end_turn(sp, B - 1)
            sp.wait_ge(y_out, 16 * (B + 1))

        @block.gpsimd
        def _(pool):
            nc.gpsimd.memset(ones_h[:], 1.0).then_inc(s_const, 1)
            nc.gpsimd.memset(eps[:], EPS).then_inc(s_const, 1)
            nc.gpsimd.memset(running[:], 0.0).then_inc(s_const, 1)
            pool.wait_ge(s_w, 16 * n_loads)
            with pool.Fori(0, B) as b:
                for i in range(NT):
                    pool.wait_ge(t_v, 2 * i + 2)
                    if i >= 2:
                        pool.wait_ge(t_o, i - 1)
                    c = CHUNK(i)
                    nc.gpsimd.tensor_scalar(rVs[i % 2][:], rV[i % 2][:], decay[:, c:c + 1], 1.0,
                                                    ALU.mult, ALU.mult).then_inc(t_vs, 1)
                pool.wait_ge(t_vs, NT)
                pool.wait_ge(turn_over, 4 * b + 4)
                pool.sem_inc(counted, 1)
                numbers = sorted(s.num for s in signals)
                assert numbers == list(range(numbers[0], numbers[-1] + 1))
                pool.sem_clear(range(numbers[0], numbers[-1] + 1))
                pool.drain().then_inc(turn_next, 1)

        @block.scalar
        def _(act):
            def transposed(layer, b):
                act.wait_ge(ln_var[layer], 1)
                nc.scalar.activation(std[:], mv[:, :, 1], ACT.Sqrt, bias=eps[:, 0:1]).then_inc(ln_std[layer], 1)
                for h in range(2):
                    act.wait_ge(xT_ps[layer], h + 1)
                    nc.scalar.copy(xT[:, h * BANK:(h + 1) * BANK], bank[h]).then_inc(xT_sb[layer], 1)

            def router_exp(layer, b):
                act.wait_ge(r_le[layer], 1)
                n = experts[layer]
                nc.scalar.activation(ex[:, :, 0:n], le[:, :, 0:n], ACT.Exp).then_inc(r_ex[layer], 1)

            def mixture(layer, b):
                todo = moe_items(layer)
                n = len(todo)

                def evacuate(i):
                    _, _, w, _ = todo[i]
                    act.wait_ge(m_t[layer], i + 1)
                    if i >= 2:
                        act.wait_ge(m_d[layer], i - 1)
                    nc.scalar.copy(hT[i % 2][:, 0:w], bank[3 + i % 2][:, 0:w]).then_inc(m_hT[layer], 1)

                for i in range(n + 2):
                    if i < n:
                        _, _, w, _ = todo[i]
                        act.wait_ge(m_gu[layer], i + 1)
                        if i >= 2:
                            act.wait_ge(m_hm[layer], i - 1)
                        nc.scalar.activation(sg[i % 2][:, 0:w], bank[i % 3][:, 0:w], ACT.Silu).then_inc(m_sg[layer], 1)
                    if i >= 2:
                        evacuate(i - 2)
                    for h in range(2):
                        if i - 2 == n // 2 * (h + 1) - 1 + (2 if h == 0 else 0):
                            act.wait_ge(m_d[layer], n // 2 * (h + 1))
                            nc.scalar.activation(gate[:, h, :], bank[5 + h], ACT.Silu).then_inc(m_g[layer], 1)

            with act.Fori(0, B) as b:
                act.wait_ge(s_w, 16 * n_loads)
                act.wait_ge(s_const, 3)
                transposed(0, b)
                for j in range(4):
                    act.wait_ge(a_proj, j + 1)
                    dst, h = (qT, kT)[j // 2], j % 2
                    nc.scalar.activation(dst[:, h * BANK:(h + 1) * BANK], bank[2 + j], ACT.Copy,
                                                 scale=float(D) ** -0.5 if j < 2 else 1.0).then_inc(a_qk, 1)
                router_exp(0, b)
                for q in range(NT):
                    act.wait_ge(a_nmx, q + 1)
                    if q >= 2:
                        act.wait_ge(a_pT, 2 * q - 2)
                    s_ps = psum[:, (q % 2) * 2 * BANK:(q % 2 + 1) * 2 * BANK]
                    nc.scalar.activation(pr[q % 2][:], s_ps, ACT.Exp, bias=nmx[:, q:q + 1],
                                                accum_out=den[:, q:q + 1]).then_inc(a_p, 1)
                    act.wait_ge(a_pT, 2 * q + 2)
                    if q >= 2:
                        act.wait_ge(a_o, q - 1)
                    nc.scalar.copy(pT[q % 2][:, BANK:], bank[5]).then_inc(a_pTa, 1)
                mixture(0, b)
                transposed(1, b)

                def silu_v(i):
                    for h in range(2):
                        act.wait_ge(t_proj, 6 * i + 5 + h)
                        if i >= 2:
                            act.wait_ge(t_vs, i - 1)
                        nc.scalar.activation(rV[i % 2][:, h * BANK:(h + 1) * BANK], bank[h], ACT.Silu).then_inc(t_v, 1)

                def silu_q(i):
                    act.wait_ge(t_rope, 4 * i + 2)
                    if i >= 2:
                        act.wait_ge(t_g, 2 * (i - 1))
                    nc.scalar.activation(rQ[i % 2][:], rp[:, 0, :], ACT.Silu).then_inc(t_q, 1)

                silu_q(0)
                silu_v(0)
                for i in range(NT):
                    for j in range(4):
                        act.wait_ge(t_t, 4 * i + j + 1)
                        dst, h = (rQT, rKT)[j % 2], j // 2
                        nc.scalar.activation(dst[:, h * BANK:(h + 1) * BANK], bank[2 + j % 2], ACT.Silu).then_inc(t_tT, 1)
                    if i + 1 < NT:
                        silu_q(i + 1)
                        silu_v(i + 1)
                    if i == 1:
                        router_exp(1, b)
                act.wait_ge(g_var, 1)
                nc.scalar.activation(gstd[:], gvar[:], ACT.Sqrt, bias=eps[:, 0:1]).then_inc(g_std, 1)
                mixture(1, b)
                end_turn(act, b)

        @block.vector
        def _(dve):
            chain = Chain(dve_done, dve)
            link = chain.link
            tt = nc.vector.tensor_tensor
            dve.wait_ge(s_w, 16 * n_loads)
            nc.vector.tensor_copy(before_h[:], before[:]).then_inc(s_const, 1)
            dve.wait_ge(s_const, 4)

            def layernorm(layer, b):
                x = xs[layer]
                for t in range(NT):
                    ins = nc.vector.bn_stats(stats[:, t, :], x[:, t, :])
                link(ins)
                for t in range(NT):
                    ins = nc.vector.bn_aggr(mv[:, t, :], stats[:, t, :])
                ins.then_inc(ln_var[layer], 1)
                dve.wait_ge(ln_std[layer], 1)
                link(nc.vector.reciprocal(rstd[:], std[:]))
                for t in range(NT):
                    nc.vector.tensor_scalar(xn[:, t, :], x[:, t, :], mv[:, t, 0:1], rstd[:, t:t + 1],
                                                            ALU.subtract, ALU.mult).then_inc(ln_xn[layer], 1)

            def router_logits(layer, b):
                n = experts[layer]
                dve.wait_ge(r_lg[layer], 1)
                ps = bank[7][:, 0:NT * n].rearrange("p (t e) -> p t e", e=n)
                if layer == 0:
                    ins = tt(lg[:, :, 0:n], ps, br0[:].unsqueeze(1).to_broadcast([P, NT, n]), ALU.add)
                else:
                    ins = nc.vector.tensor_copy(lg[:, :, 0:n], ps)
                ins.then_inc(r_ev[layer], 1)
                dve.wait_ge(r_ev[layer], 1)

            def router_choose(layer, b):
                n = experts[layer]
                for t in range(NT):
                    ins = nc.vector.max(top[:, t, :], lg[:, t, 0:n])
                link(ins)
                link(tt(le[:, :, 0:n], lg[:, :, 0:n], top[:, :, 0:1].to_broadcast([P, NT, n]), ALU.subtract))
                for t in range(NT):
                    ins = nc.vector.max_index(tix[:, t, :], top[:, t, :], lg[:, t, 0:n])
                ins.then_inc(r_le[layer], 1)
                dve.wait_ge(r_le[layer], 1)
                link(nc.vector.tensor_copy(tif[:], tix[:]))
                number = iota[:, 0:n].unsqueeze(1).to_broadcast([P, NT, n])
                for k in range((K0, K1)[layer]):
                    dst = mask if k == 0 else hot
                    link(tt(dst[:, :, 0:n], number, tif[:, :, k:k + 1].to_broadcast([P, NT, n]), ALU.is_equal))
                    if k:
                        link(tt(mask[:, :, 0:n], mask[:, :, 0:n], hot[:, :, 0:n], ALU.add))

            def router_capacity(b):
                nc.vector.tensor_copy(mask_h[:], mask[:].rearrange("p t e -> p (t e)")).then_inc(r_mask, 1)
                dve.wait_ge(r_rank, 1)
                rank = bank[6][:, 0:NT * E1].rearrange("p (t e) -> p t e", e=E1)
                link(tt(hot[:], rank, running[:].unsqueeze(1).to_broadcast([P, NT, E1]), ALU.add))
                tt(running[:], running[:], bank[6][:, NT * E1:NT * E1 + E1], ALU.add).then_inc(r_rank_read, 1)
                link(nc.vector.scalar_tensor_tensor(mask[:], hot[:], float(CAP), mask[:], ALU.is_lt, ALU.mult))
                dve.wait_ge(r_rank_read, 1)

            def router_weights(layer, b):
                n = experts[layer]
                dve.wait_ge(r_ex[layer], 1)
                if layer == 1:
                    link(nc.vector.tensor_reduce(esum[:], ex[:, :, 0:n], AX.X, ALU.add))
                link(tt(ex[:, :, 0:n], ex[:, :, 0:n], mask[:, :, 0:n], ALU.mult))
                if layer == 0:
                    link(nc.vector.tensor_reduce(esum[:], ex[:, :, 0:n], AX.X, ALU.add))
                link(nc.vector.reciprocal(rsum[:], esum[:]))
                link(tt(wt[layer][:, :, 0:n], ex[:, :, 0:n], rsum[:].unsqueeze(2).to_broadcast([P, NT, n]), ALU.mult))

            def mixture(layer, b):
                todo = moe_items(layer)
                n, f = len(todo), W[layer]
                per = GU // f
                s, x, dst = (s0, x0, x1) if layer == 0 else (ret, x1, y)
                ready = (x1_ready, y_ready)[layer]
                for i in range(n + 1):
                    if i < n:
                        t, g, w, _ = todo[i]
                        dve.wait_ge(m_sg[layer], i + 1)
                        if i >= 2:
                            dve.wait_ge(m_t[layer], i - 1)
                        tt(hm[i % 2][:, 0:w], sg[i % 2][:, 0:w], bank[i % 3][:, w:2 * w], ALU.mult).then_inc(m_hm[layer], 1)
                        if g is not None:
                            dve.wait_ge(m_hm[layer], i + 1)
                            v = lambda z: z[i % 2][:].rearrange("p (e f) -> p e f", f=f)
                            tt(v(hw), v(hm), wt[layer][:, t, g * per:(g + 1) * per].unsqueeze(2)
                                              .to_broadcast([P, per, f]), ALU.mult).then_inc(m_hw[layer], 1)
                    for h in range(2):
                        if i == (n // 2 + 4, n)[h]:
                            flat = lambda z: z[:, h * HALF:(h + 1) * HALF, :].rearrange("p t d -> p (t d)")
                            dve.wait_ge(m_g[layer], h + 1)
                            if layer == 1 and h == 0:
                                dve.wait_ge(y_out, b * 16 + 16)
                            link(tt(gs[:, h, :], gate[:, h, :], flat(s), ALU.mult))
                            tt(flat(dst), gs[:, h, :], flat(x), ALU.add).then_inc(ready, 1)
                            dve.wait_ge(ready, h + 1)

            with dve.Fori(0, B) as b:
                chain.n = 0
                dve.wait_ge(x_in, b * 16 + 16)
                layernorm(0, b)
                router_logits(0, b)
                router_choose(0, b)
                for h in range(2):
                    dve.wait_ge(a_proj, 5 + h)
                    nc.vector.tensor_copy(v0[:, h * HALF:(h + 1) * HALF, :].rearrange("p t d -> p (t d)"), bank[h]).then_inc(a_v, 1)
                router_weights(0, b)
                for q in range(NT + 1):
                    if q < NT:
                        dve.wait_ge(a_s, q + 1)
                        s_ps = psum[:, (q % 2) * 2 * BANK:(q % 2 + 1) * 2 * BANK]
                        nc.vector.tensor_reduce(nmx[:, q:q + 1], s_ps, AX.X, ALU.max, negate=True).then_inc(a_nmx, 1)
                    if q:
                        r = q - 1
                        dve.wait_ge(a_pT, 2 * r + 1)
                        if r >= 2:
                            dve.wait_ge(a_o, r - 1)
                        nc.vector.tensor_copy(pT[r % 2][:, 0:BANK], bank[4]).then_inc(a_pTd, 1)
                        dve.wait_ge(a_p, r + 1)
                        link(nc.vector.reciprocal(rden[:, r:r + 1], den[:, r:r + 1]))
                        dve.wait_ge(a_o, r + 1)
                        nc.vector.tensor_scalar(s0[:, r, :], bank[6 + r % 2][:, 0:D], rden[:, r:r + 1], None, ALU.mult).then_inc(a_od, 1)
                dve.wait_ge(a_od, NT)
                mixture(0, b)

                layernorm(1, b)
                router_logits(1, b)

                def rope(i, j):
                    c = CHUNK(i)
                    dve.wait_ge(t_proj, 6 * i + j + 1)
                    src = bank[j % 2].rearrange("p (h d) -> p h d", h=HB)
                    dst = rp[:, j // 2, (j % 2) * BANK:(j % 2 + 1) * BANK].rearrange("p (h d) -> p h d", h=HB)
                    if i:
                        if j < 2:
                            dve.wait_ge(t_q, i)
                        dve.wait_ge(t_t, 4 * i)
                    tt(dst, src, cos[:, c, :].unsqueeze(1).to_broadcast([P, HB, D]), ALU.mult)
                    swapped = bank[j % 2].rearrange("p (h i two) -> p h i two", h=HB, two=2)[:, :, 0:ROPE // 2, ::-1]
                    sn = sin[:, c, :].rearrange("p (i two) -> p i two", two=2).unsqueeze(1).to_broadcast([P, HB, ROPE // 2, 2])
                    link(tt(rsn[:].rearrange("p h (i two) -> p h i two", two=2), swapped, sn, ALU.mult))
                    tt(dst[:, :, 0:ROPE], dst[:, :, 0:ROPE], rsn[:], ALU.add).then_inc(t_rope, 1)
                    dve.wait_ge(t_rope, 4 * i + j + 1)

                def causal_part(i, h):
                    dve.wait_ge(t_a, 2 * i + h + 1)
                    if i:
                        dve.wait_ge(t_o, i)
                    tt(rA[:, h * BANK:(h + 1) * BANK].rearrange("p (h k) -> p h k", h=HB),
                               bank[4 + h].rearrange("p (h k) -> p h k", h=HB),
                               causal[:].unsqueeze(1).to_broadcast([P, HB, P]), ALU.mult).then_inc(t_am, 1)

                def add_state(i, h):
                    n = 2 * i + h + 1
                    half = slice(h * BANK, (h + 1) * BANK)
                    dve.wait_ge(t_g, n)
                    if i == 0:
                        ins = nc.vector.tensor_copy(rS[1][:, half], bank[6])
                    else:
                        dve.wait_ge(t_gs, 2 * i)
                        ins = tt(rS[(i + 1) % 2][:, half], rS[i % 2][:, half], bank[6], ALU.add)
                    ins.then_inc(t_gs, 1)

                def retained(i):
                    c = CHUNK(i)
                    dve.wait_ge(t_o, i + 1)
                    nc.vector.tensor_scalar(ret[:, c, :], bank[7][:, 0:D], undecay[:, c:c + 1], None, ALU.mult).then_inc(t_od, 1)

                for j in range(4):
                    rope(0, j)
                for i in range(NT):
                    for j in range(4):
                        if i + 1 < NT:
                            rope(i + 1, j)
                        if j < 2:
                            causal_part(i, j)
                        elif i + 1 < NT:
                            add_state(i, j - 2)
                    retained(i)
                    if i == 0:
                        router_choose(1, b)
                    if i == 1:
                        router_capacity(b)
                        router_weights(1, b)

                dve.wait_ge(t_od, NT)
                grp = lambda z: z.rearrange("p (g w) -> p g w", w=GW)
                r3 = grp(ret[:].rearrange("p t d -> p (t d)"))
                one = lambda z: z[:].unsqueeze(2).to_broadcast([P, NT * GROUPS, GW])
                link(nc.vector.tensor_reduce(gsum[:], r3, AX.X, ALU.add))
                link(nc.vector.tensor_scalar(gsum[:], gsum[:], 1.0 / GW, None, ALU.mult))
                link(tt(grp(gdev[:]), r3, one(gsum), ALU.subtract))
                link(tt(gsq[:], gdev[:], gdev[:], ALU.mult))
                link(nc.vector.tensor_reduce(gvar[:], grp(gsq[:]), AX.X, ALU.add))
                nc.vector.tensor_scalar(gvar[:], gvar[:], 1.0 / GW, None, ALU.mult).then_inc(g_var, 1)
                dve.wait_ge(g_std, 1)
                link(nc.vector.reciprocal(grs[:], gstd[:]))
                link(tt(grp(gdev[:]), grp(gdev[:]), one(grs), ALU.mult))
                tiles = lambda z: z[:].rearrange("p (t d) -> p t d", d=D)
                every = lambda z: z[:].unsqueeze(1).to_broadcast([P, NT, D])
                link(tt(ret[:], tiles(gdev), every(gnw), ALU.mult))
                link(tt(ret[:], ret[:], every(gnb), ALU.add))
                mixture(1, b)
                end_turn(dve, b)

        @block.tensor
        def _(pe):
            mm, transpose = nc.tensor.matmul, nc.tensor.transpose
            pe.wait_ge(s_w, 16 * n_loads)
            pe.wait_ge(s_const, 4)

            def columns(z, n, w=P):
                return z[:, n * w:(n + 1) * w]

            def transposed(layer, b):
                for h in range(2):
                    for t in range(HALF):
                        pe.wait_ge(ln_xn[layer], h * HALF + t + 1)
                        ins = transpose(columns(bank[h], t), xn[:, h * HALF + t, :], ident[:])
                    ins.then_inc(xT_ps[layer], 1)
                pe.wait_ge(xT_sb[layer], 2)

            def router(layer, b):
                n = experts[layer]
                for t in range(NT):
                    ins = mm(columns(bank[7], t, n), columns(xT, t), wr[layer][:], start=True, stop=True)
                ins.then_inc(r_lg[layer], 1)

            def ranks(b):
                pe.wait_ge(r_mask, 1)
                n = NT * E1
                mm(bank[6][:, 0:n], before_h[:], mask_h[:], start=True, stop=False)
                for j in range(1, NT):
                    mm(bank[6][:, j * E1:n], ones_h[:], mask_h[:, 0:n - j * E1], start=False, stop=j == NT - 1)
                for t in range(NT):
                    ins = mm(bank[6][:, n:n + E1], ones_h[:], columns(mask_h, t, E1), start=t == 0, stop=t == NT - 1)
                ins.then_inc(r_rank, 1)
                pe.wait_ge(r_rank_read, 1)

            def mixture(layer, b):
                todo = moe_items(layer)
                n = len(todo)
                weighted = 0
                for i in range(n + 3):
                    if i < n:
                        t, g, w, _ = todo[i]
                        if i >= 3:
                            pe.wait_ge(m_hm[layer], i - 2)
                        rhs = gus[:].rearrange("p u f -> p (u f)") if g is None else gu[layer][:, g, :, :].rearrange("p u f -> p (u f)")
                        mm(bank[i % 3][:, 0:2 * w], columns(xT, t), rhs, start=True, stop=True).then_inc(m_gu[layer], 1)
                    if 2 <= i < n + 2:
                        k = i - 2
                        t, g, w, _ = todo[k]
                        if g is None:
                            pe.wait_ge(m_hm[layer], k + 1)
                        else:
                            weighted += 1
                            pe.wait_ge(m_hw[layer], weighted)
                        if k >= 2:
                            pe.wait_ge(m_hT[layer], k - 1)
                        src = hm if g is None else hw
                        for j in range(w // P):
                            ins = transpose(columns(bank[3 + k % 2], j), columns(src[k % 2], j), ident[:])
                        ins.then_inc(m_t[layer], 1)
                    if i >= 3:
                        k = i - 3
                        t, g, w, last = todo[k]
                        pe.wait_ge(m_hT[layer], k + 1)
                        for j in range(w // P):
                            rhs = dns[:] if g is None else dn[layer][:, g * (GU // P) + j, :]
                            ins = mm(columns(bank[5 + t // HALF], t % HALF), columns(hT[k % 2], j), rhs,
                                     start=(g == 0 and j == 0), stop=(last and j == w // P - 1))
                        ins.then_inc(m_d[layer], 1)

            with pe.Fori(0, B) as b:
                transposed(0, b)
                router(0, b)
                for j in range(4):
                    mm(bank[2 + j], wqkv0[:, j // 2, :], columns(xT, j % 2, BANK), start=True, stop=True).then_inc(a_proj, 1)
                for h in range(2):
                    for t in range(HALF):
                        ins = mm(columns(bank[h], t), columns(xT, h * HALF + t), wqkv0[:, 2, :], start=True, stop=True)
                    ins.then_inc(a_proj, 1)

                def scores(q):
                    if q == 0:
                        pe.wait_ge(a_qk, 4)
                        pe.wait_ge(a_v, 2)
                    if q >= 2:
                        pe.wait_ge(a_p, q - 1)
                    for h in range(2):
                        ins = mm(bank[(q % 2) * 2 + h], columns(qT, q), columns(kT, h, BANK), start=True, stop=True)
                    ins.then_inc(a_s, 1)

                def attend(q):
                    pe.wait_ge(a_pTd, q + 1)
                    pe.wait_ge(a_pTa, q + 1)
                    if q == 0:
                        pe.wait_ge(r_ev[0], 1)
                    if q >= 2:
                        pe.wait_ge(a_od, q - 1)
                    for k in range(NT):
                        ins = mm(bank[6 + q % 2][:, 0:D], columns(pT[q % 2], k), v0[:, k, :], start=k == 0, stop=k == NT - 1)
                    ins.then_inc(a_o, 1)

                scores(0)
                for q in range(NT):
                    if q + 1 < NT:
                        scores(q + 1)
                    pe.wait_ge(a_p, q + 1)
                    if q:
                        pe.wait_ge(a_pTd, q)
                        pe.wait_ge(a_pTa, q)
                    for h in range(2):
                        for k in range(HALF):
                            ins = transpose(columns(bank[4 + h], k), columns(pr[q % 2], h * HALF + k), ident[:])
                        ins.then_inc(a_pT, 1)
                    if q:
                        attend(q - 1)
                attend(NT - 1)
                pe.wait_ge(a_od, NT)
                mixture(0, b)

                transposed(1, b)
                router(1, b)

                def project(i, j):
                    n = 6 * i + j
                    if n >= 2:
                        before_j = (j - 2) % 6
                        bi = i if j >= 2 else i - 1
                        if before_j >= 4:
                            pe.wait_ge(t_v, 2 * bi + before_j - 3)
                        else:
                            pe.wait_ge(t_rope, 4 * bi + before_j + 1)
                    mm(bank[j % 2], columns(xT, CHUNK(i)),
                                 wqkv1[:, j // 2, (j % 2) * BANK:(j % 2 + 1) * BANK], start=True, stop=True).then_inc(t_proj, 1)

                def transpose_half(i, j):
                    q_or_k, h = j % 2, j // 2
                    pe.wait_ge(t_rope, 4 * i + 2 * q_or_k + h + 1)
                    if 4 * i + j >= 2:
                        pe.wait_ge(t_tT, 4 * i + j - 1)
                    for k in range(HB):
                        ins = transpose(columns(bank[2 + q_or_k], k), columns(rp[:, q_or_k, :], h * HB + k), ident[:])
                    ins.then_inc(t_t, 1)

                def products(i, h):
                    pe.wait_ge(t_tT, 4 * i + 2 * h + 2)
                    if i:
                        pe.wait_ge(t_am, 2 * (i - 1) + h + 1)
                    for k in range(HB):
                        m = h * HB + k
                        ins = mm(columns(bank[4 + h], k), columns(rQT, m), columns(rKT, m), start=True, stop=True)
                    ins.then_inc(t_a, 1)

                def state(i, h):
                    n = 2 * i + h
                    pe.wait_ge(t_q, i + 1)
                    pe.wait_ge(t_vs, i + 1)
                    if n:
                        pe.wait_ge(t_gs, n)
                    for k in range(HB):
                        m = h * HB + k
                        ins = mm(columns(bank[6], k), columns(rQ[i % 2], m), columns(rVs[i % 2], m), start=True, stop=True)
                    ins.then_inc(t_g, 1)

                def across(i):
                    if i:
                        pe.wait_ge(t_gs, 2 * i)
                        pe.wait_ge(t_od, i)
                    else:
                        pe.wait_ge(r_ev[1], 1)
                        return
                    for m in range(H):
                        mm(bank[7][:, 0:D], columns(rKT, m), columns(rS[i % 2], m), start=m == 0, stop=False)

                def within(i):
                    pe.wait_ge(t_vs, i + 1)
                    pe.wait_ge(t_am, 2 * i + 2)
                    for m in range(H):
                        ins = mm(bank[7][:, 0:D], columns(rA, m), columns(rVs[i % 2], m), start=(i == 0 and m == 0), stop=m == H - 1)
                    ins.then_inc(t_o, 1)

                for j in range(6):
                    project(0, j)
                for j in range(4):
                    transpose_half(0, j)
                for i in range(NT):
                    more = i + 1 < NT
                    steps = [lambda: products(i, 0), lambda: products(i, 1),
                             lambda: more and state(i, 0), lambda: more and state(i, 1),
                             lambda: across(i), lambda: within(i)]
                    for j in range(6):
                        if more:
                            project(i + 1, j)
                        steps[j]()
                    if more:
                        for j in range(4):
                            transpose_half(i + 1, j)
                    if i == 1:
                        ranks(b)
                mixture(1, b)
                end_turn(pe, b)


_INS = ['L0_attn_X', 'L0_attn_W_Q', 'L0_attn_W_K', 'L0_attn_W_V', 'L0_ffn_router_w', 'L0_ffn_router_b',
        'L0_ffn_we_gate', 'L0_ffn_we_up', 'L0_ffn_we_down', 'L1_attn_W_Q', 'L1_attn_W_K', 'L1_attn_W_V',
        'L1_attn_gn_weight', 'L1_attn_gn_bias', 'L1_ffn_Wg', 'L1_ffn_W1', 'L1_ffn_W2', 'L1_ffn_W3',
        'L1_ffn_Ws1', 'L1_ffn_Ws2', 'L1_ffn_Ws3']


def kernel(**inputs):
    import concourse.bacc as _bacc
    from concourse.bass_utils import run_bass_kernel_spmd as _run

    nc = _bacc.Bacc("TRN2", target_bir_lowering=False, num_devices=1)
    arrays = {name: np.ascontiguousarray(inputs[name]) for name in _INS}
    arrays.update(constants())
    aps = {name: nc.dram_tensor(name, v.shape, mybir.dt.from_np(v.dtype), kind="ExternalInput").ap()
           for name, v in arrays.items()}
    out = nc.dram_tensor("out", (B, T, D), F32, kind="ExternalOutput").ap()
    two_layer_block(nc, aps, out)
    return _run(nc, [arrays], core_ids=[0]).results[0]["out"]
```

```python
import numpy as np
import concourse.bass as bass
from concourse import mybir
from contextlib import ExitStack

F32 = mybir.dt.float32
BF16 = mybir.dt.bfloat16
U32 = mybir.dt.uint32
I32 = mybir.dt.int32
ALU = mybir.AluOpType
ACT = mybir.ActivationFunctionType
AX = mybir.AxisListType

P = 128
B, T, D = 8, 1024, 128
NT = T // P
HALF = NT // 2
BANK = 512
EPS = 1e-5
E0, F0, K0 = 8, 128, 2
E1, F1, K1 = 32, 64, 4
CAP = 4 * (B * T * K1) // E1
H = 8
GAMMA = 0.96875
ROPE = 64
GROUPS = 16
GW = D // GROUPS
GRP = 4
TILES0 = -(-((T * K0 + E0 * (P - 1)) // P) // GRP) * GRP
TILES1 = -(-((T * K1 + E1 * (P - 1)) // P) // GRP) * GRP
DROP = 65536.0
YK = 16
XE, YE = 3, 3
HB = BANK // D


def constants():
    pos = np.arange(T, dtype=np.float32)
    inv = (1.0 / 10000.0 ** (np.arange(0, ROPE, 2, dtype=np.float32) / ROPE)).astype(np.float32)
    ang = np.repeat(pos[:, None] * inv[None, :], 2, axis=-1).astype(np.float64)
    cos = np.concatenate([np.cos(ang), np.ones((T, D - ROPE))], axis=1)
    sin = np.sin(ang) * np.where(np.arange(ROPE) % 2 == 0, -1.0, 1.0)
    tiles = lambda a: np.ascontiguousarray(a.reshape(NT, P, -1).transpose(1, 0, 2).astype(np.float32))
    p = np.arange(P)
    grow = GAMMA ** (np.arange(T, dtype=np.float64))
    return {
        "c_ident": np.eye(P, dtype=np.float32),
        "c_cos": tiles(cos),
        "c_sin": tiles(sin),
        "c_causal": (p[:, None] >= p[None, :]).astype(np.float32),
        "c_before": (p[:, None] < p[None, :]).astype(np.float32),
        "c_decay": tiles(grow[:, None])[:, :, 0].copy(),
        "c_undecay": tiles(1.0 / grow[:, None])[:, :, 0].copy(),
        "c_part": np.arange(P, dtype=np.float32)[:, None],
        "c_iota": np.tile(np.arange(E1, dtype=np.float32), (P, 1)),
    }


def two_layer_block(nc, a, out):
    ctx = ExitStack()
    with ctx:
        def sb(name, shape, dt=F32):
            return ctx.enter_context(nc.sbuf_tensor(name, shape, dt))

        signals = []

        def signal(name):
            signals.append(ctx.enter_context(nc.semaphore(name)))
            return signals[-1]

        class Chain:

            def __init__(self, signal, eng):
                self.sem, self.eng, self.n = signal, eng, 0

            def link(self, ins):
                self.n += 1
                ins.then_inc(self.sem, 1)
                self.eng.wait_ge(self.sem, self.n)

        ident = sb("ident", [P, P])
        cos = sb("cos", [P, NT, D])
        sin = sb("sin", [P, NT, ROPE])
        causal = sb("causal", [P, P])
        before_h = sb("before_h", [P, P], BF16)
        ones_h = sb("ones_h", [P, P], BF16)
        decay = sb("decay", [P, NT])
        undecay = sb("undecay", [P, NT])
        iota = sb("iota", [P, E1])
        part = sb("part", [P, 1])
        wqkv0 = sb("wqkv0", [P, 3, D])
        wr0 = sb("wr0", [P, E0])
        br0 = sb("br0", [P, E0])
        gu0 = sb("gu0", [P, E0, 2 * F0])
        dn0 = sb("dn0", [F0, E0, D])
        wqkv1 = sb("wqkv1", [P, 3, H * D])
        wr1 = sb("wr1", [P, E1])
        gu1 = sb("gu1", [P, E1, 2 * F1])
        dn1 = sb("dn1", [F1, E1, D])
        gus = sb("gus", [P, 2, D])
        dns = sb("dns", [P, D])
        gnw = sb("gnw", [P, D])
        gnb = sb("gnb", [P, D])

        x = [sb(f"x{i}", [P, NT, D]) for i in range(2)]
        ret = [sb(f"ret{i}", [P, NT, D]) for i in range(2)]
        z = [sb(f"z{i}", [P, NT, D]) for i in range(2)]
        yk = sb("yk", [P, YK, D])
        xn = [yk[:, 0:NT, :], sb("xn1", [P, NT, D])]
        xT = sb("xT", [P, T])
        stats = sb("stats", [P, NT, 6])
        mv = sb("mv", [P, NT, 2])
        std = sb("std", [P, NT])
        rstd = sb("rstd", [P, NT])
        eps = sb("eps", [P, 1])
        lg = sb("lg", [P, NT, E1])
        top = sb("top", [P, NT, 8])
        tix = sb("tix", [P, NT, 8], U32)
        tif = sb("tif", [P, NT, 8])
        hot = sb("hot", [P, K1, NT * E1])
        acc = sb("acc", [P, NT, D])
        pick = acc[:].rearrange("p (k t) d -> p k (t d)", k=K1)
        mask_h = sb("mask_h", [P, NT * E1], BF16)
        le = sb("le", [P, NT, E1 + K1])
        ex = sb("ex", [P, NT, E1 + K1])
        esum = sb("esum", [P, NT])
        rsum = sb("rsum", [P, NT])
        wk = [sb(f"wk{i}", [P, NT, K1]) for i in range(3)]
        running = sb("running", [P, E1])
        ranks_sb = sb("ranks_sb", [P, NT * E1 + E1])
        seen = sb("seen", [P, NT * E1])
        val = sb("val", [P, NT * E1])
        tot_i = sb("tot_i", [P, E1], I32)
        tiles_i = sb("tiles_i", [P, E1], I32)
        ntile = sb("ntile", [P, E1])
        endt = sb("endt", [P, E1])
        ones = sb("ones", [P, E1])
        base = sb("base", [P, E1])
        slot = sb("slot", [P, K1 * NT])
        over = sb("over", [P, K1 * NT])
        slots = [sb(f"slots{i}", [P, K1 * NT], I32) for i in range(3)]
        below = sb("below", [P, E1])
        ecol = sb("ecol", [P, 1])
        etab = [sb(f"etab{i}", [1, n], I32) for i, n in enumerate((TILES0, TILES1))]
        rQT = qT = sb("qT", [P, T])
        rKT = kT = sb("kT", [P, T])
        v0 = sb("v0", [P, NT, D])
        pr = [sb(f"pr{i}", [P, T]) for i in range(2)]
        pT = [sb(f"pT{i}", [P, T]) for i in range(2)]
        nmx = sb("nmx", [P, NT])
        den = sb("den", [P, NT])
        rden = sb("rden", [P, NT])
        xe = [sb(f"xe{i}", [P, GRP, D]) for i in range(XE)]
        xeT, sg, hm, hT = [sb(name, [P, 2, GRP * P]) for name in ("xeT", "sg", "hm", "hT")]
        ye = [sb(f"ye{i}", [P, GRP, D]) for i in range(YE)]
        zs = sb("zs", [P, BANK])
        zT = [sb(f"zT{i}", [P, BANK]) for i in range(2)]
        rp = sb("rp", [P, 2, H * D])
        rsn = sb("rsn", [P, HB, ROPE])
        rQ = pr
        rV = pT
        rVs = [sb(f"rVs{i}", [P, H * D]) for i in range(2)]
        rA = v0[:].rearrange("p t d -> p (t d)")
        before = sg[:, 0, 0:P]
        rS = [v[:].rearrange("p t d -> p (t d)") for v in (sg, hm)]
        gsum = sb("gsum", [P, NT * GROUPS])
        gdev = rVs[0][:]
        gsq = rVs[1][:]
        gvar = sb("gvar", [P, NT * GROUPS])
        gstd = sb("gstd", [P, NT * GROUPS])
        grs = sb("grs", [P, NT * GROUPS])

        psum = ctx.enter_context(nc.psum_tensor("psum", [P, 8 * BANK], F32))
        bank = [psum[:, i * BANK:(i + 1) * BANK] for i in range(8)]

        s_w = ctx.enter_context(nc.semaphore("s_w"))
        x_first = ctx.enter_context(nc.semaphore("x_first"))
        s_const = ctx.enter_context(nc.semaphore("s_const"))
        turn_over = ctx.enter_context(nc.semaphore("turn_over"))
        turn_next = ctx.enter_context(nc.semaphore("turn_next"))
        counted = ctx.enter_context(nc.semaphore("counted"))
        e_sent = [ctx.enter_context(nc.semaphore(f"e_sent{i}")) for i in range(2)]
        e_back = [[ctx.enter_context(nc.semaphore(f"e_back{i}_{j}")) for j in range(NT)] for i in range(2)]
        dve_done = signal("dve_done")
        x_in = signal("x_in")
        y_ready = signal("y_ready")
        y_out = signal("y_out")
        ln_var = [signal(f"ln_var{i}") for i in range(3)]
        ln_std = [signal(f"ln_std{i}") for i in range(3)]
        ln_xn = [signal(f"ln_xn{i}") for i in range(3)]
        xT_ps = [signal(f"xT_ps{i}") for i in range(2)]
        xT_sb = [signal(f"xT_sb{i}") for i in range(2)]
        r_lg = [signal(f"r_lg{i}") for i in range(2)]
        r_ev = [signal(f"r_ev{i}") for i in range(2)]
        r_le = [signal(f"r_le{i}") for i in range(2)]
        r_ex = [signal(f"r_ex{i}") for i in range(2)]
        r_mask = [signal(f"r_mask{i}") for i in range(2)]
        r_rank = [signal(f"r_rank{i}") for i in range(2)]
        r_read = [signal(f"r_read{i}") for i in range(2)]
        r_col = [signal(f"r_col{i}") for i in range(2)]
        r_row = [signal(f"r_row{i}") for i in range(2)]
        r_tab = [signal(f"r_tab{i}") for i in range(2)]
        r_slot = [signal(f"r_slot{i}") for i in range(2)]
        e_in = [signal(f"e_in{j}") for j in range(XE)]
        e_out = [signal(f"e_out{j}") for j in range(YE)]
        a_proj = signal("a_proj")
        a_qk = signal("a_qk")
        a_v = signal("a_v")
        a_s = signal("a_s")
        a_nmx = signal("a_nmx")
        a_p = signal("a_p")
        a_pT = signal("a_pT")
        a_pTd = signal("a_pTd")
        a_pTa = signal("a_pTa")
        a_o = signal("a_o")
        a_od = signal("a_od")
        m_x = signal("m_x")
        m_xT = signal("m_xT")
        m_gu = signal("m_gu")
        m_sg = signal("m_sg")
        m_hm = signal("m_hm")
        m_t = signal("m_t")
        m_hT = signal("m_hT")
        m_d = signal("m_d")
        m_y = signal("m_y")
        m_sum = [signal(f"m_sum{i}") for i in range(2)]
        m_g = [signal(f"m_g{i}") for i in range(2)]
        z_gu = signal("z_gu")
        z_s = signal("z_s")
        z_h = signal("z_h")
        z_d = signal("z_d")
        z_y = signal("z_y")
        x1_ready = signal("x1_ready")
        t_proj = signal("t_proj")
        t_rope = signal("t_rope")
        t_v = signal("t_v")
        t_vs = signal("t_vs")
        t_t = signal("t_t")
        t_tT = signal("t_tT")
        t_q = signal("t_q")
        t_a = signal("t_a")
        t_am = signal("t_am")
        t_g = signal("t_g")
        t_gs = signal("t_gs")
        t_o = signal("t_o")
        t_od = signal("t_od")
        g_var = signal("g_var")
        g_std = signal("g_std")
        ranks_ps = [bank[7], bank[6]]
        n_loads = 29
        n_tiles = [TILES0, TILES1]
        chosen = [K0, K1]
        rows_in = [nc.dram_tensor(f"rows_in{i}", (n * P, D), F32, kind="Internal").ap() for i, n in enumerate(n_tiles)]
        rows_out = [nc.dram_tensor(f"rows_out{i}", (n * P, D), F32, kind="Internal").ap() for i, n in enumerate(n_tiles)]
        rows_zero = ctx.enter_context(nc.semaphore("rows_zero"))
        n_zero = sum(n_tiles) // NT
        groups_of = lambda *layers: [(layer, i) for layer in layers for i in range(n_tiles[layer] // GRP)]
        y_store = out.rearrange("b (t p) d -> p (b t) d", p=P)
        x_load = a["L0_attn_X"].rearrange("b (t p) d -> p (b t) d", p=P)
        gu, dn, wr, experts = [gu0, gu1], [dn0, dn1], [wr0, wr1], [E0, E1]
        W = [F0, F1]
        CHUNK = lambda i: NT - 1 - i

        def gate_up_ps(work, n):
            layer, f = work[n][0], W[work[n][0]]
            ps = psum[:, BANK:3 * BANK] if layer == 0 else bank[1 + n % 2]
            return ps.rearrange("p (t u f) -> p t u f", u=2, f=f), f

        def end_turn(eng, b):
            eng.drain().then_inc(turn_over, 1)
            eng.wait_ge(turn_next, b + 1)
            eng.sem_inc(counted, 1)

        def turns(eng, turn):
            turn(0, 0, False, True)
            with eng.Fori(0, B // 2 - 1) as pair:
                turn(pair * 2 + 1, 1, True, True)
                turn(pair * 2 + 2, 0, True, True)
            turn(B - 1, 1, True, False)

        SUM0, SILU0, END0 = (12, 14), (14, 16), (15, 17)
        STATS1, ROOT1, NORM1 = 17, 19, 20

        block = ctx.enter_context(nc.Block())

        @block.sync
        def _(sp):
            loads = [
                (ident[:], a["c_ident"]), (cos[:], a["c_cos"]), (sin[:], a["c_sin"]), (causal[:], a["c_causal"]),
                (before, a["c_before"]), (decay[:], a["c_decay"]), (undecay[:], a["c_undecay"]),
                (iota[:], a["c_iota"]), (part[:], a["c_part"]),
                (wqkv0[:, 0, :], a["L0_attn_W_Q"]), (wqkv0[:, 1, :], a["L0_attn_W_K"]), (wqkv0[:, 2, :], a["L0_attn_W_V"]),
                (wr0[:], a["L0_ffn_router_w"]),
                (br0[:], a["L0_ffn_router_b"].rearrange("(o e) -> o e", o=1).to_broadcast([P, E0])),
                (wqkv1[:, 0, :], a["L1_attn_W_Q"]), (wqkv1[:, 1, :], a["L1_attn_W_K"]), (wqkv1[:, 2, :], a["L1_attn_W_V"]),
                (wr1[:], a["L1_ffn_Wg"]),
                (gus[:, 0, :], a["L1_ffn_Ws1"]), (gus[:, 1, :], a["L1_ffn_Ws3"]), (dns[:], a["L1_ffn_Ws2"]),
                (gnw[:], a["L1_attn_gn_weight"].rearrange("(o e) -> o e", o=1).to_broadcast([P, D])),
                (gnb[:], a["L1_attn_gn_bias"].rearrange("(o e) -> o e", o=1).to_broadcast([P, D])),
                (gu0[:, :, 0:F0], a["L0_ffn_we_gate"].rearrange("e d f -> d e f")),
                (gu0[:, :, F0:], a["L0_ffn_we_up"].rearrange("e d f -> d e f")),
                (dn0[:], a["L0_ffn_we_down"].rearrange("e f d -> f e d")),
                (gu1[:, :, 0:F1], a["L1_ffn_W1"].rearrange("e d f -> d e f")),
                (gu1[:, :, F1:], a["L1_ffn_W3"].rearrange("e d f -> d e f")),
                (dn1[:], a["L1_ffn_W2"].rearrange("e f d -> f e d")),
            ]
            for dst, src in loads:
                sp.dma_start(dst, src).then_inc(s_w, 16)
            n = len(loads)
            assert n == n_loads, n
            sp.wait_ge(s_const, 6)
            for rows, n in zip(rows_in, n_tiles):
                for k in range(n // NT):
                    sp.dma_start(rows[k * T:(k + 1) * T, :].rearrange("(p r) d -> p (r d)", p=P),
                                 acc[:].rearrange("p t d -> p (t d)")).then_inc(rows_zero, 16)

            def expert_rows(work, sent):
                for n, (layer, g) in enumerate(work):
                    if g == 0:
                        sp.wait_ge(e_sent[layer], sent[layer])
                    if n >= XE:
                        sp.wait_ge(m_x, n - XE + 1)
                    sp.dma_start(xe[n % XE][:], rows_in[layer][g * GRP * P:(g + 1) * GRP * P, :]
                                 .rearrange("(t p) d -> p t d", p=P)).then_inc(e_in[n % XE], 16)

            def store(b, par):
                sp.wait_ge(y_ready, 2)
                sp.dma_start(y_store[:, bass.ds(b * NT, NT), :], z[par][:]).then_inc(y_out, 16)
                sp.wait_ge(y_out, 16)

            sp.dma_start(x[0][:], x_load[:, 0:NT, :]).then_inc(x_first, 16)

            def turn(b, par, prev, more):
                expert_rows(groups_of(0, 1) if prev else groups_of(0),
                            [b * (16 * NT * K0) + 16 * NT * K0, b * (16 * NT * K1)])
                if more:
                    if prev:
                        sp.wait_ge(y_ready, 2)
                    sp.dma_start(x[1 - par][:], x_load[:, bass.ds(b * NT + NT, NT), :]).then_inc(x_in, 16)
                if prev:
                    store(b - 1, 1 - par)
                end_turn(sp, b)

            turns(sp, turn)
            expert_rows(groups_of(1), [None, B * (16 * NT * K1)])
            store(B - 1, (B - 1) % 2)

        @block.gpsimd
        def _(pool):
            nc.gpsimd.memset(ones_h[:], 1.0).then_inc(s_const, 1)
            nc.gpsimd.memset(eps[:], EPS).then_inc(s_const, 1)
            nc.gpsimd.memset(running[:], 0.0).then_inc(s_const, 1)
            nc.gpsimd.memset(acc[:], 0.0).then_inc(s_const, 1)
            nc.gpsimd.memset(ones[:], 1.0).then_inc(s_const, 1)
            pool.wait_ge(s_w, 16 * n_loads)
            pool.wait_ge(rows_zero, 16 * n_zero)

            def send(layer, par, n):
                at = slots[layer * (1 + par)]
                nc.gpsimd.indirect_dma_start(rows_in[layer], bass.IndirectOffsetOnAxis(ap=at[:, n:n + 1], axis=0),
                                             xn[layer][:, n % NT, :], None).then_inc(e_sent[layer], 16)

            def answers_stored(n):
                for j in range(YE):
                    pool.wait_ge(e_out[j], 16 * len(range(j, n, YE)))

            def fetch(layer, par, t):
                at, ring = slots[layer * (1 + par)], YK // chosen[layer]
                if t >= ring:
                    pool.wait_ge(m_sum[layer], t - ring + 1)
                for k in range(chosen[layer]):
                    n = k * NT + t
                    nc.gpsimd.indirect_dma_start(yk[:, t % ring * chosen[layer] + k, :], None, rows_out[layer],
                                                 bass.IndirectOffsetOnAxis(ap=at[:, n:n + 1], axis=0)
                                                 ).then_inc(e_back[layer][t], 16)

            def turn(b, par, prev, more):
                pool.wait_ge(r_slot[0], 1)
                for n in range(K0 * NT):
                    send(0, 0, n)
                answers_stored(len(groups_of(0)))
                for t in range(NT):
                    fetch(0, 0, t)
                if prev:
                    pool.wait_ge(x1_ready, 2)
                    answers_stored(len(groups_of(0, 1)))
                for i in range(NT):
                    pool.wait_ge(t_v, 2 * i + 2)
                    if i >= 2:
                        pool.wait_ge(t_o, i - 1)
                    c = CHUNK(i)
                    nc.gpsimd.tensor_scalar(rVs[i % 2][:], rV[i % 2][:], decay[:, c:c + 1], 1.0,
                                            ALU.mult, ALU.mult).then_inc(t_vs, 1)
                    if prev and i < NT // 2:
                        fetch(1, 1 - par, 2 * i)
                        fetch(1, 1 - par, 2 * i + 1)
                    if i >= NT // 2:
                        if i == NT // 2:
                            pool.wait_ge(r_slot[1], 1)
                        for n in range(K1 * NT // (NT // 2)):
                            send(1, par, (i - NT // 2) * (K1 * NT // (NT // 2)) + n)
                pool.wait_ge(turn_over, 4 * b + 4)
                pool.sem_inc(counted, 1)
                numbers = sorted(s.num for s in signals)
                assert numbers == list(range(numbers[0], numbers[-1] + 1))
                pool.sem_clear(range(numbers[0], numbers[-1] + 1))
                pool.drain().then_inc(turn_next, 1)

            turns(pool, turn)
            answers_stored(len(groups_of(1)))
            for t in range(NT):
                fetch(1, (B - 1) % 2, t)

        @block.scalar
        def _(act):
            def layernorm(n):
                act.wait_ge(ln_var[n], 1)
                nc.scalar.activation(std[:], mv[:, :, 1], ACT.Sqrt, bias=eps[:, 0:1]).then_inc(ln_std[n], 1)

            def transposed(layer):
                for h in range(2):
                    act.wait_ge(xT_ps[layer], h + 1)
                    nc.scalar.copy(xT[:, h * BANK:(h + 1) * BANK], bank[h]).then_inc(xT_sb[layer], 1)

            def router_exp(layer):
                act.wait_ge(r_le[layer], 1)
                lo = E1 if layer == 0 else 0
                hi = E1 + chosen[layer]
                nc.scalar.activation(ex[:, :, lo:hi], le[:, :, lo:hi], ACT.Exp).then_inc(r_ex[layer], 1)

            def mixture(work, between):
                for i in range(len(work) + 3):
                    if i < len(work):
                        act.wait_ge(m_x, i + 1)
                        if i >= 2:
                            act.wait_ge(m_gu, i - 1)
                        nc.scalar.copy(xeT[:, i % 2, :], bank[0]).then_inc(m_xT, 1)
                    if 1 <= i <= len(work):
                        k = i - 1
                        act.wait_ge(m_gu, k + 1)
                        if k >= 2:
                            act.wait_ge(m_hm, k - 1)
                        ps, f = gate_up_ps(work, k)
                        nc.scalar.activation(sg[:, k % 2, 0:GRP * f].rearrange("p (t f) -> p t f", f=f),
                                             ps[:, :, 0, :], ACT.Silu).then_inc(m_sg, 1)
                    if i >= 3:
                        k = i - 3
                        layer, g = work[k]
                        act.wait_ge(m_d, k + 1)
                        if k >= YE:
                            act.wait_ge(e_out[k % YE], 16 * (k // YE))
                        nc.scalar.copy(ye[k % YE][:].rearrange("p t d -> p (t d)"), bank[4 + k % 2]).then_inc(m_y, 1)
                        act.wait_ge(m_y, k + 1)
                        act.dma_start(rows_out[layer][g * GRP * P:(g + 1) * GRP * P, :].rearrange("(t p) d -> p t d", p=P),
                                      ye[k % YE][:]).then_inc(e_out[k % YE], 16)
                    between(i)

            def mixture_silu(layer, h):
                act.wait_ge(m_sum[layer], (h + 1) * HALF)
                half = acc[:, h * HALF:(h + 1) * HALF, :]
                nc.scalar.activation(half, half, ACT.Silu).then_inc(m_g[layer], 1)

            def shared(par):
                for h in range(2):
                    act.wait_ge(z_gu, h + 1)
                    if h:
                        act.wait_ge(z_h, h)
                    nc.scalar.activation(zs[:], bank[2 + 2 * h], ACT.Silu).then_inc(z_s, 1)
                for h in range(2):
                    act.wait_ge(z_d, h + 1)
                    nc.scalar.copy(z[par][:, h * HALF:(h + 1) * HALF, :].rearrange("p t d -> p (t d)"),
                                   bank[6 + h]).then_inc(z_y, 1)

            def group_norm():
                act.wait_ge(g_var, 1)
                nc.scalar.activation(gstd[:], gvar[:], ACT.Sqrt, bias=eps[:, 0:1]).then_inc(g_std, 1)

            def silu_v(i):
                for h in range(2):
                    act.wait_ge(t_proj, 6 * i + 5 + h)
                    if i >= 2:
                        act.wait_ge(t_vs, i - 1)
                    nc.scalar.activation(rV[i % 2][:, h * BANK:(h + 1) * BANK], bank[h], ACT.Silu).then_inc(t_v, 1)

            def silu_q(i):
                act.wait_ge(t_rope, 4 * i + 2)
                if i >= 2:
                    act.wait_ge(t_g, 2 * (i - 1))
                nc.scalar.activation(rQ[i % 2][:], rp[:, 0, :], ACT.Silu).then_inc(t_q, 1)

            act.wait_ge(s_w, 16 * n_loads)
            act.wait_ge(s_const, 6)
            layernorm(2)

            def turn(b, par, prev, more):
                transposed(0)
                for j in range(4):
                    act.wait_ge(a_proj, j + 1)
                    dst, h = (qT, kT)[j // 2], j % 2
                    nc.scalar.activation(dst[:, h * BANK:(h + 1) * BANK], bank[2 + j], ACT.Copy,
                                         scale=float(D) ** -0.5 if j < 2 else 1.0).then_inc(a_qk, 1)
                if prev:
                    group_norm()
                for q in range(NT):
                    act.wait_ge(a_nmx, q + 1)
                    if q >= 2:
                        act.wait_ge(a_pT, 2 * q - 2)
                    s_ps = psum[:, (q % 2) * 2 * BANK:(q % 2 + 1) * 2 * BANK]
                    nc.scalar.activation(pr[q % 2][:], s_ps, ACT.Exp, bias=nmx[:, q:q + 1],
                                         accum_out=den[:, q:q + 1]).then_inc(a_p, 1)
                    act.wait_ge(a_pT, 2 * q + 2)
                    if q >= 2:
                        act.wait_ge(a_o, q - 1)
                    nc.scalar.copy(pT[q % 2][:, BANK:], bank[5]).then_inc(a_pTa, 1)
                    if q == 2:
                        router_exp(0)
                if prev:
                    def between(i):
                        if i in SILU0:
                            mixture_silu(0, SILU0.index(i))
                        if i == ROOT1:
                            layernorm(1)
                    mixture(groups_of(0, 1), between)
                else:
                    mixture(groups_of(0), lambda i: None)
                    mixture_silu(0, 0)
                    mixture_silu(0, 1)
                    layernorm(1)
                transposed(1)
                shared(par)
                silu_q(0)
                silu_v(0)
                for i in range(NT):
                    for j in range(4):
                        act.wait_ge(t_t, 4 * i + j + 1)
                        dst, h = (rQT, rKT)[j % 2], j // 2
                        nc.scalar.activation(dst[:, h * BANK:(h + 1) * BANK], bank[2 + j % 2], ACT.Silu).then_inc(t_tT, 1)
                    if i + 1 < NT:
                        silu_q(i + 1)
                        silu_v(i + 1)
                    if i == 1:
                        router_exp(1)
                    if prev and i in (3, 5):
                        mixture_silu(1, (i - 3) // 2)
                if more:
                    layernorm(0)
                end_turn(act, b)

            turns(act, turn)
            group_norm()
            mixture(groups_of(1), lambda i: None)
            mixture_silu(1, 0)
            mixture_silu(1, 1)

        @block.vector
        def _(dve):
            chain = Chain(dve_done, dve)
            link = chain.link
            tt = nc.vector.tensor_tensor
            dve.wait_ge(s_w, 16 * n_loads)
            nc.vector.tensor_copy(before_h[:], before).then_inc(s_const, 1)
            dve.wait_ge(s_const, 6)

            def ln_stats(n, src):
                for t in range(NT):
                    ins = nc.vector.bn_stats(stats[:, t, :], src[:, t, :])
                link(ins)
                for t in range(NT):
                    ins = nc.vector.bn_aggr(mv[:, t, :], stats[:, t, :])
                ins.then_inc(ln_var[n], 1)

            def ln_norm(n, src):
                dve.wait_ge(ln_std[n], 1)
                link(nc.vector.reciprocal(rstd[:], std[:]))
                for t in range(NT):
                    nc.vector.tensor_scalar(xn[n % 2][:, t, :], src[:, t, :], mv[:, t, 0:1], rstd[:, t:t + 1],
                                            ALU.subtract, ALU.mult).then_inc(ln_xn[n], 1)

            def router_logits(layer, b):
                n = experts[layer]
                dve.wait_ge(r_lg[layer], 1)
                ps = bank[7][:, 0:NT * n].rearrange("p (t e) -> p t e", e=n)
                if layer == 0:
                    ins = tt(lg[:, :, 0:n], ps, br0[:].unsqueeze(1).to_broadcast([P, NT, n]), ALU.add)
                else:
                    ins = nc.vector.tensor_copy(lg[:, :, 0:n], ps)
                ins.then_inc(r_ev[layer], 1)
                dve.wait_ge(r_ev[layer], 1)

            def router_choose(layer, b):
                n, k = experts[layer], chosen[layer]
                for t in range(NT):
                    ins = nc.vector.max(top[:, t, :], lg[:, t, 0:n])
                link(ins)
                largest = top[:, :, 0:1]
                if layer == 1:
                    tt(le[:, :, 0:n], lg[:, :, 0:n], largest.to_broadcast([P, NT, n]), ALU.subtract)
                tt(le[:, :, E1:E1 + k], top[:, :, 0:k], largest.to_broadcast([P, NT, k]), ALU.subtract).then_inc(r_le[layer], 1)
                for t in range(NT):
                    ins = nc.vector.max_index(tix[:, t, :], top[:, t, :], lg[:, t, 0:n])
                link(ins)
                link(nc.vector.tensor_copy(tif[:], tix[:]))
                link(tt(hot[:, 0:k, 0:NT * n].rearrange("p k (t e) -> p k t e", e=n),
                        iota[:, 0:n].unsqueeze(1).unsqueeze(1).to_broadcast([P, k, NT, n]),
                        tif[:, :, 0:k].rearrange("p t k -> p k t").unsqueeze(3).to_broadcast([P, k, NT, n]), ALU.is_equal))
                m = NT * n
                if k == 2:
                    tt(mask_h[:, 0:m], hot[:, 0, 0:m], hot[:, 1, 0:m], ALU.add).then_inc(r_mask[layer], 1)
                else:
                    link(tt(pick[:, 0:2, 0:m], hot[:, 0:2, 0:m], hot[:, 2:4, 0:m], ALU.add))
                    tt(mask_h[:, 0:m], pick[:, 0, 0:m], pick[:, 1, 0:m], ALU.add).then_inc(r_mask[layer], 1)

            def router_slots(layer, par):
                n, k = experts[layer], chosen[layer]
                m = NT * n
                dve.wait_ge(r_rank[layer], 1)
                nc.vector.tensor_copy(ranks_sb[:, 0:m + n], ranks_ps[layer][:, 0:m + n]).then_inc(r_read[layer], 1)
                dve.wait_ge(r_read[layer], 1)
                total = ranks_sb[:, m:m + n]
                link(nc.vector.tensor_scalar(tot_i[:, 0:n], total, float(P - 1), None, ALU.add))
                link(nc.vector.tensor_single_scalar(tiles_i[:, 0:n], tot_i[:, 0:n], 7, ALU.logical_shift_right))
                link(nc.vector.tensor_copy(ntile[:, 0:n], tiles_i[:, 0:n]))
                link(nc.vector.tensor_tensor_scan(endt[:, 0:n], ones[:, 0:n], ntile[:, 0:n], 0.0, ALU.mult, ALU.add))
                link(nc.vector.tensor_scalar(below[:, 0:n], endt[:, 0:n], part[:, 0:1], None, ALU.is_le))
                link(nc.vector.tensor_reduce(ecol[:], below[:, 0:n], AX.X, ALU.add))
                nc.vector.tensor_scalar(ecol[:], ecol[:], float(n - 1), None, ALU.min).then_inc(r_col[layer], 1)
                link(tt(base[:, 0:n], endt[:, 0:n], ntile[:, 0:n], ALU.subtract))
                rank = ranks_sb[:, 0:m].rearrange("p (t e) -> p t e", e=n)
                tiled = lambda v: v[:, 0:n].unsqueeze(1).to_broadcast([P, NT, n])
                wide = lambda v: v[:, 0:m].rearrange("p (t e) -> p t e", e=n)
                last = nc.vector.scalar_tensor_tensor(wide(val), tiled(base), float(P), rank, ALU.mult, ALU.add)
                if layer == 1:
                    link(tt(wide(seen), rank, tiled(running), ALU.add))
                    link(nc.vector.tensor_scalar(seen[:], seen[:], float(CAP), DROP, ALU.is_ge, ALU.mult))
                    link(tt(val[:], val[:], seen[:], ALU.add))
                    last = tt(running[:], running[:], total, ALU.add)
                link(last)
                link(tt(pick[:, 0:k, 0:m], hot[:, 0:k, 0:m], val[:, 0:m].unsqueeze(1).to_broadcast([P, k, m]), ALU.mult))
                link(nc.vector.tensor_reduce(slot[:, 0:k * NT].rearrange("p (k t) -> p k t", k=k),
                                             pick[:, 0:k, 0:m].rearrange("p k (t e) -> p k t e", e=n), AX.X, ALU.add))
                if layer == 1:
                    link(nc.vector.tensor_scalar(over[:], slot[:], DROP, None, ALU.is_ge))
                    nc.vector.scalar_tensor_tensor(slots[1 + par][:], over[:], -DROP, slot[:], ALU.mult, ALU.add).then_inc(r_slot[1], 1)
                else:
                    nc.vector.tensor_copy(slots[0][:, 0:k * NT], slot[:, 0:k * NT]).then_inc(r_slot[0], 1)

            def router_weights(layer, par):
                n, k = experts[layer], chosen[layer]
                dve.wait_ge(r_ex[layer], 1)
                among = ex[:, :, E1:E1 + k] if layer == 0 else ex[:, :, 0:n]
                link(nc.vector.tensor_reduce(esum[:], among, AX.X, ALU.add))
                link(nc.vector.reciprocal(rsum[:], esum[:]))
                w = wk[layer * (1 + par)][:, :, 0:k]
                link(tt(w, ex[:, :, E1:E1 + k], rsum[:].unsqueeze(2).to_broadcast([P, NT, k]), ALU.mult))
                if layer == 1:
                    dve.wait_ge(r_slot[1], 1)
                    link(nc.vector.tensor_scalar(over[:], over[:], -1.0, 1.0, ALU.mult, ALU.add))
                    link(tt(w, w, over[:].rearrange("p (k t) -> p t k", k=k), ALU.mult))

            def expert_table(layer):
                dve.wait_ge(r_row[layer], 1)
                nc.vector.tensor_scalar(etab[layer][:], ranks_ps[layer][0:1, 0:n_tiles[layer]], float(D), None,
                                        ALU.mult).then_inc(r_tab[layer], 1)

            def mixture(work, between):
                for i in range(len(work) + 1):
                    if i < len(work):
                        dve.wait_ge(m_sg, i + 1)
                        if i >= 2:
                            dve.wait_ge(m_t, i - 1)
                        ps, f = gate_up_ps(work, i)
                        v = lambda q: q[:, i % 2, 0:GRP * f].rearrange("p (t f) -> p t f", f=f)
                        tt(v(hm), v(sg), ps[:, :, 1, :], ALU.mult).then_inc(m_hm, 1)
                    if i:
                        k = i - 1
                        f = W[work[k][0]]
                        dve.wait_ge(m_t, k + 1)
                        if k >= 2:
                            dve.wait_ge(m_d, k - 1)
                        nc.vector.tensor_copy(hT[0:f, k % 2, :], bank[3][0:f, :]).then_inc(m_hT, 1)
                    between(i)

            def sum_tiles(layer, par, h, back):
                for t in range(h * HALF, (h + 1) * HALF):
                    sum_tile(layer, par, t, back)

            def sum_tile(layer, par, t, back):
                k = chosen[layer]
                dve.wait_ge(e_back[layer][t], back)
                for j in range(k):
                    w = wk[layer * (1 + par)][:, t, j:j + 1]
                    src = yk[:, t % (YK // k) * k + j, :]
                    if j == 0 and layer == 0:
                        ins = nc.vector.tensor_scalar(acc[:, t, :], src, w, None, ALU.mult)
                    else:
                        ins = nc.vector.scalar_tensor_tensor(acc[:, t, :], src, w, z[par][:, t, :] if j == 0 else acc[:, t, :],
                                                             ALU.mult, ALU.add)
                    if j < k - 1:
                        link(ins)
                ins.then_inc(m_sum[layer], 1)

            def end_block(layer, par, h):
                half = lambda v: v[:, h * HALF:(h + 1) * HALF, :]
                s, dst, ready = (z, x, x1_ready) if layer == 0 else (ret, z, y_ready)
                dve.wait_ge(m_g[layer], h + 1)
                link(tt(half(acc), half(acc), half(s[par]), ALU.mult))
                tt(half(dst[par]), half(acc), half(x[par]), ALU.add).then_inc(ready, 1)
                dve.wait_ge(ready, h + 1)

            def shared():
                for h in range(2):
                    dve.wait_ge(z_s, h + 1)
                    tt(zT[h][:], zs[:], bank[3 + 2 * h], ALU.mult).then_inc(z_h, 1)

            def group_norm_1(par):
                r3 = grp(ret[par][:].rearrange("p t d -> p (t d)"))
                link(nc.vector.tensor_reduce(gsum[:], r3, AX.X, ALU.add))
                link(nc.vector.tensor_scalar(gsum[:], gsum[:], 1.0 / GW, None, ALU.mult))
                link(tt(grp(gdev), r3, one(gsum), ALU.subtract))
                link(tt(gsq, gdev, gdev, ALU.mult))
                link(nc.vector.tensor_reduce(gvar[:], grp(gsq), AX.X, ALU.add))
                nc.vector.tensor_scalar(gvar[:], gvar[:], 1.0 / GW, None, ALU.mult).then_inc(g_var, 1)

            def group_norm_2(par):
                dve.wait_ge(g_std, 1)
                link(nc.vector.reciprocal(grs[:], gstd[:]))
                link(tt(grp(gdev), grp(gdev), one(grs), ALU.mult))
                link(tt(ret[par][:], gdev.rearrange("p (t d) -> p t d", d=D), every(gnw), ALU.mult))
                link(tt(ret[par][:], ret[par][:], every(gnb), ALU.add))

            grp = lambda v: v.rearrange("p (g w) -> p g w", w=GW)
            one = lambda v: v[:].unsqueeze(2).to_broadcast([P, NT * GROUPS, GW])
            every = lambda v: v[:].unsqueeze(1).to_broadcast([P, NT, D])

            def rope(i, j):
                c = CHUNK(i)
                dve.wait_ge(t_proj, 6 * i + j + 1)
                src = bank[j % 2].rearrange("p (h d) -> p h d", h=HB)
                dst = rp[:, j // 2, (j % 2) * BANK:(j % 2 + 1) * BANK].rearrange("p (h d) -> p h d", h=HB)
                if i:
                    if j < 2:
                        dve.wait_ge(t_q, i)
                    dve.wait_ge(t_t, 4 * i)
                tt(dst, src, cos[:, c, :].unsqueeze(1).to_broadcast([P, HB, D]), ALU.mult)
                swapped = bank[j % 2].rearrange("p (h i two) -> p h i two", h=HB, two=2)[:, :, 0:ROPE // 2, ::-1]
                sn = sin[:, c, :].rearrange("p (i two) -> p i two", two=2).unsqueeze(1).to_broadcast([P, HB, ROPE // 2, 2])
                link(tt(rsn[:].rearrange("p h (i two) -> p h i two", two=2), swapped, sn, ALU.mult))
                tt(dst[:, :, 0:ROPE], dst[:, :, 0:ROPE], rsn[:], ALU.add).then_inc(t_rope, 1)
                dve.wait_ge(t_rope, 4 * i + j + 1)

            def causal_part(i, h):
                dve.wait_ge(t_a, 2 * i + h + 1)
                if i:
                    dve.wait_ge(t_o, i)
                tt(rA[:, h * BANK:(h + 1) * BANK].rearrange("p (h k) -> p h k", h=HB),
                   bank[4 + h].rearrange("p (h k) -> p h k", h=HB),
                   causal[:].unsqueeze(1).to_broadcast([P, HB, P]), ALU.mult).then_inc(t_am, 1)

            def add_state(i, h):
                n = 2 * i + h + 1
                half = slice(h * BANK, (h + 1) * BANK)
                dve.wait_ge(t_g, n)
                if i == 0:
                    ins = nc.vector.tensor_copy(rS[1][:, half], bank[6])
                else:
                    dve.wait_ge(t_gs, 2 * i)
                    ins = tt(rS[(i + 1) % 2][:, half], rS[i % 2][:, half], bank[6], ALU.add)
                ins.then_inc(t_gs, 1)

            def retained(i, par):
                c = CHUNK(i)
                dve.wait_ge(t_o, i + 1)
                nc.vector.tensor_scalar(ret[par][:, c, :], bank[7][:, 0:D], undecay[:, c:c + 1], None, ALU.mult).then_inc(t_od, 1)

            dve.wait_ge(x_first, 16)
            ln_stats(2, x[0])
            ln_norm(2, x[0])

            def turn(b, par, prev, more):
                if prev:
                    group_norm_1(1 - par)
                router_logits(0, b)
                for h in range(2):
                    dve.wait_ge(a_proj, 5 + h)
                    nc.vector.tensor_copy(v0[:, h * HALF:(h + 1) * HALF, :].rearrange("p t d -> p (t d)"), bank[h]).then_inc(a_v, 1)
                for q in range(NT + 2):
                    if q < NT:
                        dve.wait_ge(a_s, q + 1)
                        s_ps = psum[:, (q % 2) * 2 * BANK:(q % 2 + 1) * 2 * BANK]
                        nc.vector.tensor_reduce(nmx[:, q:q + 1], s_ps, AX.X, ALU.max, negate=True).then_inc(a_nmx, 1)
                    if 1 <= q <= NT:
                        r = q - 1
                        dve.wait_ge(a_pT, 2 * r + 1)
                        if r >= 2:
                            dve.wait_ge(a_o, r - 1)
                        nc.vector.tensor_copy(pT[r % 2][:, 0:BANK], bank[4]).then_inc(a_pTd, 1)
                        dve.wait_ge(a_p, r + 1)
                        link(nc.vector.reciprocal(rden[:, r:r + 1], den[:, r:r + 1]))
                    if q >= 2:
                        r = q - 2
                        dve.wait_ge(a_o, r + 1)
                        nc.vector.tensor_scalar(z[par][:, r, :], bank[6][:, 0:D], rden[:, r:r + 1], None, ALU.mult).then_inc(a_od, 1)
                    if q == 0:
                        router_choose(0, b)
                    if q == 2:
                        router_slots(0, 0)
                    if q == 3:
                        expert_table(0)
                        router_weights(0, 0)
                    if q == 5 and prev:
                        group_norm_2(1 - par)
                dve.wait_ge(a_od, NT)
                back0 = b * (16 * K0) + 16 * K0
                if prev:
                    def between(i):
                        if i in SUM0:
                            sum_tiles(0, 0, SUM0.index(i), back0)
                        if i in END0:
                            end_block(0, par, END0.index(i))
                        if i == STATS1:
                            ln_stats(1, x[par])
                        if i == NORM1:
                            ln_norm(1, x[par])
                    mixture(groups_of(0, 1), between)
                else:
                    mixture(groups_of(0), lambda i: None)
                    sum_tiles(0, 0, 0, back0)
                    sum_tiles(0, 0, 1, back0)
                    end_block(0, par, 0)
                    end_block(0, par, 1)
                    ln_stats(1, x[par])
                    ln_norm(1, x[par])

                router_logits(1, b)
                shared()
                for j in range(4):
                    rope(0, j)
                for i in range(NT):
                    for j in range(4):
                        if i + 1 < NT:
                            rope(i + 1, j)
                        if j < 2:
                            causal_part(i, j)
                        elif i + 1 < NT:
                            add_state(i, j - 2)
                    retained(i, par)
                    if i == 0:
                        router_choose(1, b)
                    if i == 1:
                        router_slots(1, par)
                        router_weights(1, par)
                    if i == 2:
                        expert_table(1)
                    if prev and i in (2, 4):
                        sum_tiles(1, 1 - par, (i - 2) // 2, b * (16 * K1))
                    if prev and i in (4, 6):
                        end_block(1, 1 - par, (i - 4) // 2)
                if more:
                    dve.wait_ge(x_in, 16)
                    ln_stats(0, x[1 - par])
                    ln_norm(0, x[1 - par])
                end_turn(dve, b)
                chain.n = 0

            turns(dve, turn)
            group_norm_1((B - 1) % 2)
            group_norm_2((B - 1) % 2)
            mixture(groups_of(1), lambda i: None)
            for h in range(2):
                sum_tiles(1, (B - 1) % 2, h, B * (16 * K1))
                end_block(1, (B - 1) % 2, h)

        @block.tensor
        def _(pe):
            mm, transpose = nc.tensor.matmul, nc.tensor.transpose
            pe.wait_ge(s_w, 16 * n_loads)
            pe.wait_ge(s_const, 6)

            def columns(z, n, w=P):
                return z[:, n * w:(n + 1) * w]

            def transposed(layer, ln=None):
                for h in range(2):
                    for t in range(HALF):
                        if ln is not None:
                            pe.wait_ge(ln, h * HALF + t + 1)
                        ins = transpose(columns(bank[h], t), xn[layer][:, h * HALF + t, :], ident[:])
                    ins.then_inc(xT_ps[layer], 1)
                pe.wait_ge(xT_sb[layer], 2)

            def router(layer, b):
                n = experts[layer]
                for t in range(NT):
                    ins = mm(columns(bank[7], t, n), columns(xT, t), wr[layer][:], start=True, stop=True)
                ins.then_inc(r_lg[layer], 1)

            def ranks(layer, b):
                n = experts[layer]
                m = NT * n
                pe.wait_ge(r_mask[layer], 1)
                mm(ranks_ps[layer][:, 0:m], before_h[:], mask_h[:, 0:m], start=True, stop=False)
                for j in range(1, NT):
                    mm(ranks_ps[layer][:, j * n:m], ones_h[:], mask_h[:, 0:m - j * n], start=False, stop=j == NT - 1)
                for t in range(NT):
                    ins = mm(ranks_ps[layer][:, m:m + n], ones_h[:], columns(mask_h, t, n), start=t == 0, stop=t == NT - 1)
                ins.then_inc(r_rank[layer], 1)

            def expert_row(layer):
                n = n_tiles[layer]
                pe.wait_ge(r_read[layer], 1)
                pe.wait_ge(r_col[layer], 1)
                mm(ranks_ps[layer][0:1, 0:n], ecol[:], ident[:, 0:n], start=True, stop=True).then_inc(r_row[layer], 1)

            def mixture(work):
                expert = {}

                def read_experts(i):
                    layer, g = work[i]
                    _, expert[i] = nc.values_load_multi_w_load_instructions(
                        etab[layer][0:1, g * GRP:(g + 1) * GRP], engines=[mybir.EngineType.PE], min_val=0,
                        max_val=(experts[layer] - 1) * D,
                        skip_runtime_bounds_check_because="router_slots keeps every tile's expert within the experts")

                def rows(i):
                    pe.wait_ge(e_in[i % XE], 16 * (i // XE + 1))
                    if i:
                        pe.wait_ge(m_xT, i)
                    for t in range(GRP):
                        ins = transpose(columns(bank[0], t), xe[i % XE][:, t, :], ident[:])
                    ins.then_inc(m_x, 1)

                def gate_and_up(i):
                    layer, g = work[i]
                    pe.wait_ge(m_xT, i + 1)
                    ring = 1 if 0 in (layer, work[i - 1][0]) else 2
                    if i >= ring:
                        pe.wait_ge(m_hm, i - ring + 1)
                    f = W[layer]
                    ps = psum[:, BANK:3 * BANK] if layer == 0 else bank[1 + i % 2]
                    weights = gu[layer][:].rearrange("p e f -> p (e f)")
                    for t in range(GRP):
                        at = expert[i][t] * 2 if layer == 0 else expert[i][t]
                        ins = mm(columns(ps, t, 2 * f), columns(xeT[:, i % 2, :], t), weights[:, bass.ds(at, 2 * f)],
                                 start=True, stop=True)
                    ins.then_inc(m_gu, 1)

                def hidden(i):
                    f = W[work[i][0]]
                    pe.wait_ge(m_hm, i + 1)
                    if i:
                        pe.wait_ge(m_hT, i)
                    for t in range(GRP):
                        ins = transpose(columns(bank[3], t)[0:f, :], columns(hm[:, i % 2, :], t, f), ident[:])
                    ins.then_inc(m_t, 1)

                def answers(i):
                    layer, g = work[i]
                    f = W[layer]
                    pe.wait_ge(m_hT, i + 1)
                    if i >= 2:
                        pe.wait_ge(m_y, i - 1)
                    weights = dn[layer][:].rearrange("p e d -> p (e d)")
                    for t in range(GRP):
                        ins = mm(columns(bank[4 + i % 2], t), columns(hT[0:f, i % 2, :], t),
                                 weights[:, bass.ds(expert[i][t], D)], start=True, stop=True)
                    ins.then_inc(m_d, 1)

                read_experts(0)
                for i in range(len(work) + 3):
                    if i < len(work):
                        rows(i)
                    if 2 <= i < len(work) + 2:
                        hidden(i - 2)
                    if 1 <= i <= len(work):
                        gate_and_up(i - 1)
                    if i >= 3:
                        answers(i - 3)
                    if i + 1 < len(work):
                        read_experts(i + 1)

            def shared():
                for h in range(2):
                    mm(bank[2 + 2 * h], gus[:, 0, :], columns(xT, h, BANK), start=True, stop=True)
                    mm(bank[3 + 2 * h], gus[:, 1, :], columns(xT, h, BANK), start=True, stop=True).then_inc(z_gu, 1)
                pe.wait_ge(r_ev[1], 1)
                for h in range(2):
                    pe.wait_ge(z_h, h + 1)
                    for t in range(HALF):
                        ins = mm(columns(bank[6 + h], t), columns(zT[h], t), dns[:], start=True, stop=True)
                    ins.then_inc(z_d, 1)

            def turn(b, par, prev, more):
                transposed(0, None if prev else ln_xn[2])
                router(0, b)
                for j in range(4):
                    mm(bank[2 + j], wqkv0[:, j // 2, :], columns(xT, j % 2, BANK), start=True, stop=True).then_inc(a_proj, 1)
                for h in range(2):
                    for t in range(HALF):
                        ins = mm(columns(bank[h], t), columns(xT, h * HALF + t), wqkv0[:, 2, :], start=True, stop=True)
                    ins.then_inc(a_proj, 1)

                def scores(q):
                    if q == 0:
                        pe.wait_ge(a_qk, 4)
                        pe.wait_ge(a_v, 2)
                    if q >= 2:
                        pe.wait_ge(a_p, q - 1)
                    for h in range(2):
                        ins = mm(bank[(q % 2) * 2 + h], columns(qT, q), columns(kT, h, BANK), start=True, stop=True)
                    ins.then_inc(a_s, 1)

                def attend(q):
                    pe.wait_ge(a_pTd, q + 1)
                    pe.wait_ge(a_pTa, q + 1)
                    if q == 1:
                        expert_row(0)
                    if q:
                        pe.wait_ge(a_od, q)
                    for k in range(NT):
                        ins = mm(bank[6][:, 0:D], columns(pT[q % 2], k), v0[:, k, :], start=k == 0, stop=k == NT - 1)
                    ins.then_inc(a_o, 1)

                scores(0)
                for q in range(NT):
                    if q + 1 < NT:
                        scores(q + 1)
                    pe.wait_ge(a_p, q + 1)
                    if q:
                        pe.wait_ge(a_pTd, q)
                        pe.wait_ge(a_pTa, q)
                    for h in range(2):
                        for k in range(HALF):
                            ins = transpose(columns(bank[4 + h], k), columns(pr[q % 2], h * HALF + k), ident[:])
                        ins.then_inc(a_pT, 1)
                    if q == 0:
                        ranks(0, b)
                    if q:
                        attend(q - 1)
                attend(NT - 1)
                pe.wait_ge(a_od, NT)
                pe.wait_ge(r_tab[0], 1)
                mixture(groups_of(0, 1) if prev else groups_of(0))
                transposed(1, ln_xn[1])
                router(1, b)
                shared()

                def project(i, j):
                    n = 6 * i + j
                    if n >= 2:
                        before_j = (j - 2) % 6
                        bi = i if j >= 2 else i - 1
                        if before_j >= 4:
                            pe.wait_ge(t_v, 2 * bi + before_j - 3)
                        else:
                            pe.wait_ge(t_rope, 4 * bi + before_j + 1)
                    mm(bank[j % 2], columns(xT, CHUNK(i)),
                                 wqkv1[:, j // 2, (j % 2) * BANK:(j % 2 + 1) * BANK], start=True, stop=True).then_inc(t_proj, 1)

                def transpose_half(i, j):
                    q_or_k, h = j % 2, j // 2
                    pe.wait_ge(t_rope, 4 * i + 2 * q_or_k + h + 1)
                    if 4 * i + j >= 2:
                        pe.wait_ge(t_tT, 4 * i + j - 1)
                    for k in range(HB):
                        ins = transpose(columns(bank[2 + q_or_k], k), columns(rp[:, q_or_k, :], h * HB + k), ident[:])
                    ins.then_inc(t_t, 1)

                def products(i, h):
                    pe.wait_ge(t_tT, 4 * i + 2 * h + 2)
                    if i:
                        pe.wait_ge(t_am, 2 * (i - 1) + h + 1)
                    for k in range(HB):
                        m = h * HB + k
                        ins = mm(columns(bank[4 + h], k), columns(rQT, m), columns(rKT, m), start=True, stop=True)
                    ins.then_inc(t_a, 1)

                def state(i, h):
                    n = 2 * i + h
                    pe.wait_ge(t_q, i + 1)
                    pe.wait_ge(t_vs, i + 1)
                    if n:
                        pe.wait_ge(t_gs, n)
                    if i == 2 and h == 0:
                        pe.wait_ge(r_read[1], 1)
                    if i == 3 and h == 0:
                        pe.wait_ge(r_tab[1], 1)
                    for k in range(HB):
                        m = h * HB + k
                        ins = mm(columns(bank[6], k), columns(rQ[i % 2], m), columns(rVs[i % 2], m), start=True, stop=True)
                    ins.then_inc(t_g, 1)

                def across(i):
                    if i:
                        pe.wait_ge(t_gs, 2 * i)
                        pe.wait_ge(t_od, i)
                    else:
                        pe.wait_ge(r_ev[1], 1)
                        return
                    for m in range(H):
                        mm(bank[7][:, 0:D], columns(rKT, m), columns(rS[i % 2], m), start=m == 0, stop=False)

                def within(i):
                    pe.wait_ge(t_vs, i + 1)
                    pe.wait_ge(t_am, 2 * i + 2)
                    for m in range(H):
                        ins = mm(bank[7][:, 0:D], columns(rA, m), columns(rVs[i % 2], m), start=(i == 0 and m == 0), stop=m == H - 1)
                    ins.then_inc(t_o, 1)

                for j in range(6):
                    project(0, j)
                pe.wait_ge(z_y, 2)
                for j in range(4):
                    transpose_half(0, j)
                for i in range(NT):
                    more = i + 1 < NT
                    steps = [lambda: products(i, 0), lambda: products(i, 1),
                             lambda: more and state(i, 0), lambda: more and state(i, 1),
                             lambda: across(i), lambda: within(i)]
                    for j in range(6):
                        if more:
                            project(i + 1, j)
                        steps[j]()
                    if more:
                        for j in range(4):
                            transpose_half(i + 1, j)
                    if i == 1:
                        pe.wait_ge(t_gs, 4)
                        ranks(1, b)
                    if i == 2:
                        pe.wait_ge(t_gs, 6)
                        expert_row(1)
                end_turn(pe, b)

            turns(pe, turn)
            mixture(groups_of(1))


_INS = ['L0_attn_X', 'L0_attn_W_Q', 'L0_attn_W_K', 'L0_attn_W_V', 'L0_ffn_router_w', 'L0_ffn_router_b',
        'L0_ffn_we_gate', 'L0_ffn_we_up', 'L0_ffn_we_down', 'L1_attn_W_Q', 'L1_attn_W_K', 'L1_attn_W_V',
        'L1_attn_gn_weight', 'L1_attn_gn_bias', 'L1_ffn_Wg', 'L1_ffn_W1', 'L1_ffn_W2', 'L1_ffn_W3',
        'L1_ffn_Ws1', 'L1_ffn_Ws2', 'L1_ffn_Ws3']


def kernel(**inputs):
    import concourse.bacc as _bacc
    from concourse.bass_utils import run_bass_kernel_spmd as _run

    nc = _bacc.Bacc("TRN2", target_bir_lowering=False, num_devices=1)
    arrays = {name: np.ascontiguousarray(inputs[name]) for name in _INS}
    arrays.update(constants())
    aps = {name: nc.dram_tensor(name, v.shape, mybir.dt.from_np(v.dtype), kind="ExternalInput").ap()
           for name, v in arrays.items()}
    out = nc.dram_tensor("out", (B, T, D), F32, kind="ExternalOutput").ap()
    two_layer_block(nc, aps, out)
    return _run(nc, [arrays], core_ids=[0]).results[0]["out"]
```

```python
import numpy as np
import concourse.bass as bass
from concourse import mybir
from contextlib import ExitStack

F32 = mybir.dt.float32
F32R = mybir.dt.float32r
BF16 = mybir.dt.bfloat16
U32 = mybir.dt.uint32
I32 = mybir.dt.int32
ALU = mybir.AluOpType
ACT = mybir.ActivationFunctionType
AX = mybir.AxisListType

P = 128
B, T, D = 8, 1024, 128
NT = T // P
HALF = NT // 2
BANK = 512
EPS = 1e-5
E0, F0, K0 = 8, 128, 2
E1, F1, K1 = 32, 64, 4
CAP = 4 * (B * T * K1) // E1
H = 8
GAMMA = 0.96875
ROPE = 64
GROUPS = 16
GW = D // GROUPS
GRP = 4
TILES0 = -(-((T * K0 + E0 * (P - 1)) // P) // GRP) * GRP
TILES1 = -(-((T * K1 + E1 * (P - 1)) // P) // GRP) * GRP
DROP = 65536.0
YK = 16
XE, YE = 3, 3
HB = BANK // D


def constants():
    pos = np.arange(T, dtype=np.float32)
    inv = (1.0 / 10000.0 ** (np.arange(0, ROPE, 2, dtype=np.float32) / ROPE)).astype(np.float32)
    ang = np.repeat(pos[:, None] * inv[None, :], 2, axis=-1).astype(np.float64)
    cos = np.cos(ang)
    sin = np.sin(ang) * np.where(np.arange(ROPE) % 2 == 0, -1.0, 1.0)
    tiles = lambda a: np.ascontiguousarray(a.reshape(NT, P, -1).transpose(1, 0, 2).astype(np.float32))
    p = np.arange(P)
    grow = GAMMA ** (np.arange(T, dtype=np.float64))
    return {
        "c_ident": np.eye(P, dtype=np.float32),
        "c_cos": tiles(cos),
        "c_sin": tiles(sin),
        "c_causal": (p[:, None] >= p[None, :]).astype(np.float32),
        "c_before": (p[:, None] < p[None, :]).astype(np.float32),
        "c_decay": tiles(grow[:, None])[:, :, 0].copy(),
        "c_undecay": tiles(1.0 / grow[:, None])[:, :, 0].copy(),
        "c_part": np.arange(P, dtype=np.float32)[:, None],
        "c_iota": np.tile(np.arange(E1, dtype=np.float32), (P, 1)),
    }


def two_layer_block(nc, a, out):
    ctx = ExitStack()
    with ctx:
        def sb(name, shape, dt=F32):
            return ctx.enter_context(nc.sbuf_tensor(name, shape, dt))

        signals = []

        def signal(name):
            signals.append(ctx.enter_context(nc.semaphore(name)))
            return signals[-1]

        class Chain:

            def __init__(self, signal, eng):
                self.sem, self.eng, self.n = signal, eng, 0

            def link(self, ins):
                self.n += 1
                ins.then_inc(self.sem, 1)
                self.eng.wait_ge(self.sem, self.n)

        ident = sb("ident", [P, P])
        cos = sb("cos", [P, NT, ROPE])
        sin = sb("sin", [P, NT, ROPE])
        causal = sb("causal", [P, P])
        before_h = sb("before_h", [P, P], BF16)
        ones_h = sb("ones_h", [P, P], BF16)
        decay = sb("decay", [P, NT])
        undecay = sb("undecay", [P, NT])
        iota = sb("iota", [P, E1])
        part = sb("part", [P, 1])
        wqkv0 = sb("wqkv0", [P, 3, D])
        wr0 = sb("wr0", [P, E0])
        br0 = sb("br0", [P, E0])
        gu0 = sb("gu0", [P, E0, 2 * F0])
        dn0 = sb("dn0", [F0, E0, D])
        w1_hi = sb("w1_hi", [P, 3, H * D], F32R)
        w1_lo = sb("w1_lo", [P, 3, H * D], F32R)
        wr1 = sb("wr1", [P, E1])
        gu1 = sb("gu1", [P, E1, 2 * F1])
        dn1 = sb("dn1", [F1, E1, D])
        gus = sb("gus", [P, 2, D])
        dns = sb("dns", [P, D])
        gnw = sb("gnw", [P, D])
        gnb = sb("gnb", [P, D])

        x = [sb(f"x{i}", [P, NT, D]) for i in range(2)]
        ret = [sb(f"ret{i}", [P, NT, D]) for i in range(2)]
        z = [sb(f"z{i}", [P, NT, D]) for i in range(2)]
        yk = sb("yk", [P, YK, D])
        xn = [yk[:, 0:NT, :], sb("xn1", [P, NT, D])]
        xT = sb("xT", [P, T])
        stats = sb("stats", [P, NT, 6])
        mv = sb("mv", [P, NT, 2])
        std = sb("std", [P, NT])
        rstd = sb("rstd", [P, NT])
        eps = sb("eps", [P, 1])
        lg = sb("lg", [P, NT, E1])
        top = sb("top", [P, NT, 8])
        tix = sb("tix", [P, NT, 8], U32)
        tif = sb("tif", [P, NT, 8])
        hot = sb("hot", [P, K1, NT * E1])
        pick = sb("pick", [P, K1, NT * E1])
        acc = sb("acc", [P, NT, D])
        mask_h = sb("mask_h", [P, NT * E1], BF16)
        le = sb("le", [P, NT, E1 + K1])
        ex = le
        esum = sb("esum", [P, NT])
        rsum = sb("rsum", [P, NT])
        wk = [sb(f"wk{i}", [P, NT, K1]) for i in range(3)]
        running = sb("running", [P, E1])
        ranks_sb = sb("ranks_sb", [P, NT * E1 + E1])
        seen = lg[:].rearrange("p t e -> p (t e)")
        val = sb("val", [P, NT * E1])
        tot_i = sb("tot_i", [P, E1], I32)
        tiles_i = sb("tiles_i", [P, E1], I32)
        ntile = sb("ntile", [P, E1])
        endt = sb("endt", [P, E1])
        ones = sb("ones", [P, E1])
        base = sb("base", [P, E1])
        slot = sb("slot", [P, K1 * NT])
        over = sb("over", [P, K1 * NT])
        slots = [sb(f"slots{i}", [P, K1 * NT], I32) for i in range(3)]
        below = sb("below", [P, E1])
        ecol = sb("ecol", [P, 1])
        etab = [sb(f"etab{i}", [1, n], I32) for i, n in enumerate((TILES0, TILES1))]
        rQT = qT = sb("qT", [P, T])
        rKT = kT = sb("kT", [P, T])
        v0 = sb("v0", [P, NT, D])
        pr = [sb(f"pr{i}", [P, T]) for i in range(2)]
        pT = [sb(f"pT{i}", [P, T]) for i in range(2)]
        nmx = sb("nmx", [P, NT])
        den = sb("den", [P, NT])
        rden = sb("rden", [P, NT])
        xe = [sb(f"xe{i}", [P, GRP, D]) for i in range(XE)]
        xeT, sg, hm, hT = [sb(name, [P, 2, GRP * P]) for name in ("xeT", "sg", "hm", "hT")]
        ye = [sb(f"ye{i}", [P, GRP, D]) for i in range(YE)]
        zs = sg[:, 0, :]
        zT = [hm[:, i, :] for i in range(2)]
        rp = sb("rp", [P, 2, H * D])
        x_hi = sb("x_hi", [P, 2, P], F32R)
        x_lo = sb("x_lo", [P, 2, P], F32R)
        wqkv1 = [v[:].rearrange("p t d -> p (t d)") for v in (ret[0], ret[1], z[1])]
        rsn = sb("rsn", [P, HB, ROPE])
        rQ = pr
        rV = pT
        rA = v0[:].rearrange("p t d -> p (t d)")
        before = sg[:, 0, 0:P]
        rS = [v[:].rearrange("p t d -> p (t d)") for v in (sg, hm)]
        gsum = sb("gsum", [P, NT * GROUPS])
        g_beside = [v[:].rearrange("p t d -> p (t d)") for v in (sg, hm)]
        g_behind = [rQT[:], rKT[:]]
        gvar = sb("gvar", [P, NT * GROUPS])
        gstd = sb("gstd", [P, NT * GROUPS])
        grs = sb("grs", [P, NT * GROUPS])

        psum = ctx.enter_context(nc.psum_tensor("psum", [P, 8 * BANK], F32))
        bank = [psum[:, i * BANK:(i + 1) * BANK] for i in range(8)]

        s_w = [ctx.enter_context(nc.semaphore(f"s_w{i}")) for i in range(3)]
        x_first = ctx.enter_context(nc.semaphore("x_first"))
        s_const = ctx.enter_context(nc.semaphore("s_const"))
        turn_over = ctx.enter_context(nc.semaphore("turn_over"))
        turn_next = ctx.enter_context(nc.semaphore("turn_next"))
        counted = ctx.enter_context(nc.semaphore("counted"))
        e_sent = [ctx.enter_context(nc.semaphore(f"e_sent{i}")) for i in range(2)]
        e_back = [[ctx.enter_context(nc.semaphore(f"e_back{i}_{j}")) for j in range(NT)] for i in range(2)]
        dve_done = signal("dve_done")
        x_in = signal("x_in")
        y_ready = signal("y_ready")
        y_out = signal("y_out")
        ln_var = [signal(f"ln_var{i}") for i in range(3)]
        ln_std = [signal(f"ln_std{i}") for i in range(3)]
        ln_xn = [signal(f"ln_xn{i}") for i in range(3)]
        xT_ps = [signal(f"xT_ps{i}") for i in range(2)]
        xT_sb = [signal(f"xT_sb{i}") for i in range(2)]
        r_lg = [signal(f"r_lg{i}") for i in range(2)]
        r_ev = [signal(f"r_ev{i}") for i in range(2)]
        r_le = [signal(f"r_le{i}") for i in range(2)]
        r_ex = [signal(f"r_ex{i}") for i in range(2)]
        r_mask = [signal(f"r_mask{i}") for i in range(2)]
        r_rank = [signal(f"r_rank{i}") for i in range(2)]
        r_read = [signal(f"r_read{i}") for i in range(2)]
        r_col = [signal(f"r_col{i}") for i in range(2)]
        r_row = [signal(f"r_row{i}") for i in range(2)]
        r_tab = [signal(f"r_tab{i}") for i in range(2)]
        r_slot = [signal(f"r_slot{i}") for i in range(2)]
        e_in = [signal(f"e_in{j}") for j in range(XE)]
        e_out = [signal(f"e_out{j}") for j in range(YE)]
        a_proj = signal("a_proj")
        a_qk = signal("a_qk")
        a_v = signal("a_v")
        a_s = signal("a_s")
        a_nmx = signal("a_nmx")
        a_p = signal("a_p")
        a_pT = signal("a_pT")
        a_pTd = signal("a_pTd")
        a_pTa = signal("a_pTa")
        a_o = signal("a_o")
        a_od = signal("a_od")
        m_x = signal("m_x")
        m_xT = signal("m_xT")
        m_gu = signal("m_gu")
        m_sg = signal("m_sg")
        m_hm = signal("m_hm")
        m_t = signal("m_t")
        m_hT = signal("m_hT")
        m_d = signal("m_d")
        m_y = signal("m_y")
        m_sum = [signal(f"m_sum{i}") for i in range(2)]
        m_g = [signal(f"m_g{i}") for i in range(2)]
        z_gu = signal("z_gu")
        z_s = signal("z_s")
        z_h = signal("z_h")
        z_d = signal("z_d")
        z_y = signal("z_y")
        x1_ready = signal("x1_ready")
        w_hi = signal("w_hi")
        w_lo = signal("w_lo")
        t_hi = signal("t_hi")
        t_lo = signal("t_lo")
        t_proj = signal("t_proj")
        t_rope = signal("t_rope")
        t_raw = signal("t_raw")
        t_v = signal("t_v")
        t_vs = signal("t_vs")
        t_t = signal("t_t")
        t_tT = signal("t_tT")
        t_q = signal("t_q")
        t_a = signal("t_a")
        t_am = signal("t_am")
        t_g = signal("t_g")
        t_gs = signal("t_gs")
        t_o = signal("t_o")
        t_od = signal("t_od")
        g_var = signal("g_var")
        g_std = signal("g_std")
        ranks_ps = bank[7]
        product_bank = lambda i, h: 0 if (i, h) == (NT - 1, 1) else 4
        n_loads = [9, 3, 17]
        n_tiles = [TILES0, TILES1]
        chosen = [K0, K1]
        rows_in = [nc.dram_tensor(f"rows_in{i}", (n * P, D), F32, kind="Internal").ap() for i, n in enumerate(n_tiles)]
        rows_out = [nc.dram_tensor(f"rows_out{i}", (n * P, D), F32, kind="Internal").ap() for i, n in enumerate(n_tiles)]
        rows_zero = [ctx.enter_context(nc.semaphore(f"rows_zero{i}")) for i in range(2)]
        groups_of = lambda *layers: [(layer, i) for layer in layers for i in range(n_tiles[layer] // GRP)]
        y_store = out.rearrange("b (t p) d -> p (b t) d", p=P)
        x_load = a["L0_attn_X"].rearrange("b (t p) d -> p (b t) d", p=P)
        gu, dn, wr, experts = [gu0, gu1], [dn0, dn1], [wr0, wr1], [E0, E1]
        W = [F0, F1]
        CHUNK = lambda i: NT - 1 - i

        def gate_up_ps(work, n):
            layer = work[n][0]
            f = W[layer]
            first = 1 + n % 2 if layer else (1, 6)[n % 2]
            ps = psum[:, first * BANK:(first + GRP * 2 * f // BANK) * BANK]
            return ps, ps.rearrange("p (t u f) -> p t u f", u=2, f=f)

        def end_turn(eng, b):
            eng.drain().then_inc(turn_over, 1)
            eng.wait_ge(turn_next, b + 1)
            eng.sem_inc(counted, 1)

        def turns(eng, turn):
            turn(0, 0, False, True)
            with eng.Fori(0, B // 2 - 1) as pair:
                turn(pair * 2 + 1, 1, True, True)
                turn(pair * 2 + 2, 0, True, True)
            turn(B - 1, 1, True, False)

        PAIRS = [(t, t + 1) for t in range(0, NT, 2)]
        SUM0, SILU0, END0 = (12, 13, 14, 15), (15, 17), (16, 18)
        STATS1, ROOT1, NORM1 = (17, 19), 22, 22
        SUM1, SILU1, END1 = ((2, 0), (2, 3), (3, 2), (4, 1)), (3, 4), ((4, 2), (5, 2))
        STATS0, NORM0 = (NT - 2, 3), (NT - 1, 2)

        block = ctx.enter_context(nc.Block())

        @block.sync
        def _(sp):
            broadcast = lambda v, n: v.rearrange("(o e) -> o e", o=1).to_broadcast([P, n])
            loads = [
                [(ident[:], a["c_ident"]),
                 (wr0[:], a["L0_ffn_router_w"]), (br0[:], broadcast(a["L0_ffn_router_b"], E0)),
                 (wqkv0[:, 0, :], a["L0_attn_W_Q"]), (wqkv0[:, 1, :], a["L0_attn_W_K"]), (wqkv0[:, 2, :], a["L0_attn_W_V"]),
                 (before, a["c_before"]), (iota[:], a["c_iota"]), (part[:], a["c_part"])],
                [(gu0[:, :, 0:F0], a["L0_ffn_we_gate"].rearrange("e d f -> d e f")),
                 (gu0[:, :, F0:], a["L0_ffn_we_up"].rearrange("e d f -> d e f")),
                 (dn0[:], a["L0_ffn_we_down"].rearrange("e f d -> f e d"))],
                [(wr1[:], a["L1_ffn_Wg"]),
                 (gus[:, 0, :], a["L1_ffn_Ws1"]), (gus[:, 1, :], a["L1_ffn_Ws3"]), (dns[:], a["L1_ffn_Ws2"]),
                 (wqkv1[0], a["L1_attn_W_Q"]), (wqkv1[1], a["L1_attn_W_K"]), (wqkv1[2], a["L1_attn_W_V"]),
                 (cos[:], a["c_cos"]), (sin[:], a["c_sin"]), (causal[:], a["c_causal"]),
                 (decay[:], a["c_decay"]), (undecay[:], a["c_undecay"]),
                 (gnw[:], broadcast(a["L1_attn_gn_weight"], D)), (gnb[:], broadcast(a["L1_attn_gn_bias"], D)),
                 (gu1[:, :, 0:F1], a["L1_ffn_W1"].rearrange("e d f -> d e f")),
                 (gu1[:, :, F1:], a["L1_ffn_W3"].rearrange("e d f -> d e f")),
                 (dn1[:], a["L1_ffn_W2"].rearrange("e f d -> f e d"))],
            ]
            assert [len(v) for v in loads] == n_loads
            sp.dma_start(x[0][:], x_load[:, 0:NT, :]).then_inc(x_first, 16)
            for n, part_loads in enumerate(loads):
                for dst, src in part_loads:
                    sp.dma_start(dst, src).then_inc(s_w[n], 16)
                if n == 1:
                    sp.wait_ge(s_const, 6)
                if n:
                    for k in range(n_tiles[n - 1] // NT):
                        sp.dma_start(rows_in[n - 1][k * T:(k + 1) * T, :].rearrange("(p r) d -> p (r d)", p=P),
                                     acc[:].rearrange("p t d -> p (t d)")).then_inc(rows_zero[n - 1], 16)

            def expert_rows(work, sent):
                for n, (layer, g) in enumerate(work):
                    if g == 0:
                        sp.wait_ge(e_sent[layer], sent[layer])
                    if n >= XE:
                        sp.wait_ge(m_x, n - XE + 1)
                    sp.dma_start(xe[n % XE][:], rows_in[layer][g * GRP * P:(g + 1) * GRP * P, :]
                                 .rearrange("(t p) d -> p t d", p=P)).then_inc(e_in[n % XE], 16)

            def store(b, par):
                sp.wait_ge(y_ready, 2)
                sp.dma_start(y_store[:, bass.ds(b * NT, NT), :], z[par][:]).then_inc(y_out, 16)
                sp.wait_ge(y_out, 16)

            def turn(b, par, prev, more):
                expert_rows(groups_of(0, 1) if prev else groups_of(0),
                            [b * (16 * NT * K0) + 16 * NT * K0, b * (16 * NT * K1)])
                if more:
                    if prev:
                        sp.wait_ge(y_ready, 2)
                    sp.dma_start(x[1 - par][:], x_load[:, bass.ds(b * NT + NT, NT), :]).then_inc(x_in, 16)
                if prev:
                    store(b - 1, 1 - par)
                end_turn(sp, b)

            turns(sp, turn)
            expert_rows(groups_of(1), [None, B * (16 * NT * K1)])
            store(B - 1, (B - 1) % 2)

        @block.gpsimd
        def _(pool):
            nc.gpsimd.memset(ones_h[:], 1.0).then_inc(s_const, 1)
            nc.gpsimd.memset(eps[:], EPS).then_inc(s_const, 1)
            nc.gpsimd.memset(running[:], 0.0).then_inc(s_const, 1)
            nc.gpsimd.memset(acc[:], 0.0).then_inc(s_const, 1)
            nc.gpsimd.memset(ones[:], 1.0).then_inc(s_const, 1)

            def send(layer, par, n):
                at = slots[layer * (1 + par)]
                nc.gpsimd.indirect_dma_start(rows_in[layer], bass.IndirectOffsetOnAxis(ap=at[:, n:n + 1], axis=0),
                                             xn[layer][:, n % NT, :], None).then_inc(e_sent[layer], 16)

            def answers_stored(n):
                for j in range(YE):
                    pool.wait_ge(e_out[j], 16 * len(range(j, n, YE)))

            def fetch(layer, par, t):
                at, ring = slots[layer * (1 + par)], YK // chosen[layer]
                if t >= ring:
                    pool.wait_ge(m_sum[layer], t - ring + 1)
                for k in range(chosen[layer]):
                    n = k * NT + t
                    nc.gpsimd.indirect_dma_start(yk[:, t % ring * chosen[layer] + k, :], None, rows_out[layer],
                                                 bass.IndirectOffsetOnAxis(ap=at[:, n:n + 1], axis=0)
                                                 ).then_inc(e_back[layer][t], 16)

            def turn(b, par, prev, more):
                pool.wait_ge(r_slot[0], 1)
                if not prev:
                    pool.wait_ge(rows_zero[0], 16 * (TILES0 // NT))
                for n in range(K0 * NT):
                    send(0, 0, n)
                answers_stored(len(groups_of(0)))
                for t in range(NT):
                    fetch(0, 0, t)
                if prev:
                    pool.wait_ge(x1_ready, 2)
                    answers_stored(len(groups_of(0, 1)))
                    for t in range(NT):
                        fetch(1, 1 - par, t)
                pool.wait_ge(r_slot[1], 1)
                if not prev:
                    pool.wait_ge(rows_zero[1], 16 * (TILES1 // NT))
                for n in range(K1 * NT):
                    send(1, par, n)
                pool.wait_ge(turn_over, 4 * b + 4)
                pool.sem_inc(counted, 1)
                numbers = sorted(s.num for s in signals)
                assert numbers == list(range(numbers[0], numbers[-1] + 1))
                pool.sem_clear(range(numbers[0], numbers[-1] + 1))
                pool.drain().then_inc(turn_next, 1)

            turns(pool, turn)
            answers_stored(len(groups_of(1)))
            for t in range(NT):
                fetch(1, (B - 1) % 2, t)

        @block.scalar
        def _(act):
            def layernorm(n):
                act.wait_ge(ln_var[n], 1)
                nc.scalar.activation(std[:], mv[:, :, 1], ACT.Sqrt, bias=eps[:, 0:1]).then_inc(ln_std[n], 1)

            def transposed(layer):
                for h in range(2):
                    act.wait_ge(xT_ps[layer], h + 1)
                    nc.scalar.copy(xT[:, h * BANK:(h + 1) * BANK], bank[h]).then_inc(xT_sb[layer], 1)

            def router_exp(layer):
                act.wait_ge(r_le[layer], 1)
                lo = E1 if layer == 0 else 0
                hi = E1 + chosen[layer]
                nc.scalar.activation(ex[:, :, lo:hi], le[:, :, lo:hi], ACT.Exp).then_inc(r_ex[layer], 1)

            def mixture(work, between):
                for i in range(len(work) + 3):
                    if i < len(work):
                        act.wait_ge(m_x, i + 1)
                        if i >= 2:
                            act.wait_ge(m_gu, i - 1)
                        nc.scalar.copy(xeT[:, i % 2, :], bank[0]).then_inc(m_xT, 1)
                    if 1 <= i <= len(work):
                        k = i - 1
                        act.wait_ge(m_gu, k + 1)
                        if k >= 2:
                            act.wait_ge(m_hm, k - 1)
                        ps, f = gate_up_ps(work, k)[1], W[work[k][0]]
                        nc.scalar.activation(sg[:, k % 2, 0:GRP * f].rearrange("p (t f) -> p t f", f=f),
                                             ps[:, :, 0, :], ACT.Silu).then_inc(m_sg, 1)
                    if i >= 3:
                        k = i - 3
                        layer, g = work[k]
                        act.wait_ge(m_d, k + 1)
                        if k >= YE:
                            act.wait_ge(e_out[k % YE], 16 * (k // YE))
                        nc.scalar.copy(ye[k % YE][:].rearrange("p t d -> p (t d)"), bank[4 + k % 2]).then_inc(m_y, 1)
                        act.wait_ge(m_y, k + 1)
                        act.dma_start(rows_out[layer][g * GRP * P:(g + 1) * GRP * P, :].rearrange("(t p) d -> p t d", p=P),
                                      ye[k % YE][:]).then_inc(e_out[k % YE], 16)
                    between(i)

            def mixture_silu(layer, h):
                act.wait_ge(m_sum[layer], (h + 1) * HALF)
                half = acc[:, h * HALF:(h + 1) * HALF, :]
                nc.scalar.activation(half, half, ACT.Silu).then_inc(m_g[layer], 1)

            def shared(par):
                for h in range(2):
                    act.wait_ge(z_gu, h + 1)
                    if h:
                        act.wait_ge(z_h, h)
                    nc.scalar.activation(zs, bank[2 + 2 * h], ACT.Silu).then_inc(z_s, 1)
                for h in range(2):
                    act.wait_ge(z_d, h + 1)
                    nc.scalar.copy(z[par][:, h * HALF:(h + 1) * HALF, :].rearrange("p t d -> p (t d)"),
                                   bank[6 + h]).then_inc(z_y, 1)

            def group_norm():
                act.wait_ge(g_var, 1)
                nc.scalar.activation(gstd[:], gvar[:], ACT.Sqrt, bias=eps[:, 0:1]).then_inc(g_std, 1)

            def silu_v(i):
                if i >= 2:
                    act.wait_ge(t_o, i - 1)
                for h in range(2):
                    act.wait_ge(t_proj, 6 * i + 5 + h)
                    nc.scalar.activation(rV[i % 2][:, h * BANK:(h + 1) * BANK], bank[h], ACT.Silu).then_inc(t_v, 1)
                act.wait_ge(t_v, 2 * i + 2)
                c = CHUNK(i)
                nc.scalar.activation(rV[i % 2][:], rV[i % 2][:], ACT.Copy, scale=decay[:, c:c + 1]).then_inc(t_vs, 1)

            def chunk_hi(i):
                if i >= 2:
                    act.wait_ge(t_proj, 6 * (i - 1))
                c = CHUNK(i)
                nc.scalar.copy(x_hi[:, i % 2, :], xT[:, c * P:(c + 1) * P]).then_inc(t_hi, 1)

            def take_half(i, j):
                act.wait_ge(t_proj, 6 * i + j + 1)
                if i:
                    act.wait_ge(t_t, 4 * (i - 1) + (1, 3, 2, 4)[j])
                    act.wait_ge(t_q, i)
                nc.scalar.copy(rp[:, j // 2, (j % 2) * BANK:(j % 2 + 1) * BANK], bank[j % 2]).then_inc(t_raw, 1)

            def silu_q(i):
                act.wait_ge(t_rope, 4 * i + 2)
                if i >= 2:
                    act.wait_ge(t_g, 2 * (i - 1))
                nc.scalar.activation(rQ[i % 2][:], rp[:, 0, :], ACT.Silu).then_inc(t_q, 1)

            act.wait_ge(s_const, 6)
            layernorm(2)

            def turn(b, par, prev, more):
                transposed(0)
                for j in range(4):
                    act.wait_ge(a_proj, j + 1)
                    dst, h = (qT, kT)[j // 2], j % 2
                    nc.scalar.activation(dst[:, h * BANK:(h + 1) * BANK], bank[2 + j], ACT.Copy,
                                         scale=float(D) ** -0.5 if j < 2 else 1.0).then_inc(a_qk, 1)
                if prev:
                    group_norm()
                for q in range(NT):
                    act.wait_ge(a_nmx, q + 1)
                    if q >= 2:
                        act.wait_ge(a_pT, 2 * q - 2)
                    s_ps = psum[:, (q % 2) * 2 * BANK:(q % 2 + 1) * 2 * BANK]
                    nc.scalar.activation(pr[q % 2][:], s_ps, ACT.Exp, bias=nmx[:, q:q + 1],
                                         accum_out=den[:, q:q + 1]).then_inc(a_p, 1)
                    act.wait_ge(a_pT, 2 * q + 2)
                    if q >= 2:
                        act.wait_ge(a_o, q - 1)
                    nc.scalar.copy(pT[q % 2][:, BANK:], bank[5]).then_inc(a_pTa, 1)
                    if q == 2:
                        router_exp(0)
                if prev:
                    def between(i):
                        if i in SILU0:
                            mixture_silu(0, SILU0.index(i))
                        if i == ROOT1:
                            layernorm(1)
                    mixture(groups_of(0, 1), between)
                else:
                    mixture(groups_of(0), lambda i: None)
                    mixture_silu(0, 0)
                    mixture_silu(0, 1)
                    layernorm(1)
                transposed(1)
                act.wait_ge(xT_sb[1], 2)
                chunk_hi(0)
                chunk_hi(1)
                if not prev:
                    act.wait_ge(s_w[2], 16 * n_loads[2])
                    for j in range(3):
                        nc.scalar.copy(w1_hi[:, j, :], wqkv1[j]).then_inc(w_hi, 1)
                    act.wait_ge(w_lo, 3)
                shared(par)
                for j in range(4):
                    take_half(0, j)
                silu_v(0)
                silu_q(0)
                for i in range(NT):
                    if i + 2 < NT:
                        chunk_hi(i + 2)
                    for j in range(4):
                        act.wait_ge(t_t, 4 * i + j + 1)
                        dst, h = (rQT, rKT)[j % 2], j // 2
                        nc.scalar.activation(dst[:, h * BANK:(h + 1) * BANK], bank[2 + j % 2], ACT.Silu).then_inc(t_tT, 1)
                        if j == 1 and i + 1 < NT:
                            take_half(i + 1, 0)
                    if i + 1 < NT:
                        for j in range(1, 4):
                            take_half(i + 1, j)
                        silu_v(i + 1)
                        silu_q(i + 1)
                    if i == 1:
                        router_exp(1)
                    if prev and i in SILU1:
                        mixture_silu(1, SILU1.index(i))
                if more:
                    layernorm(0)
                end_turn(act, b)

            turns(act, turn)
            group_norm()
            mixture(groups_of(1), lambda i: None)
            mixture_silu(1, 0)
            mixture_silu(1, 1)

        @block.vector
        def _(dve):
            chain = Chain(dve_done, dve)
            link = chain.link
            tt = nc.vector.tensor_tensor
            dve.wait_ge(s_w[0], 16 * n_loads[0])
            nc.vector.tensor_copy(before_h[:], before).then_inc(s_const, 1)
            dve.wait_ge(s_const, 6)

            def ln_stats_half(src, h):
                for t in range(h * HALF, (h + 1) * HALF):
                    ins = nc.vector.bn_stats(stats[:, t, :], src[:, t, :])
                return ins

            def ln_stats(n, src, first=True):
                if first:
                    ln_stats_half(src, 0)
                link(ln_stats_half(src, 1))
                for t in range(NT):
                    ins = nc.vector.bn_aggr(mv[:, t, :], stats[:, t, :])
                ins.then_inc(ln_var[n], 1)

            def ln_norm(n, src):
                dve.wait_ge(ln_std[n], 1)
                link(nc.vector.reciprocal(rstd[:], std[:]))
                for t in range(NT):
                    nc.vector.tensor_scalar(xn[n % 2][:, t, :], src[:, t, :], mv[:, t, 0:1], rstd[:, t:t + 1],
                                            ALU.subtract, ALU.mult).then_inc(ln_xn[n], 1)

            def router_logits(layer, b):
                n = experts[layer]
                dve.wait_ge(r_lg[layer], 1)
                ps = bank[7][:, 0:NT * n].rearrange("p (t e) -> p t e", e=n)
                if layer == 0:
                    ins = tt(lg[:, :, 0:n], ps, br0[:].unsqueeze(1).to_broadcast([P, NT, n]), ALU.add)
                else:
                    ins = nc.vector.tensor_copy(lg[:, :, 0:n], ps)
                ins.then_inc(r_ev[layer], 1)
                dve.wait_ge(r_ev[layer], 1)

            def router_choose(layer, b):
                n, k = experts[layer], chosen[layer]
                for t in range(NT):
                    ins = nc.vector.max(top[:, t, :], lg[:, t, 0:n])
                link(ins)
                largest = top[:, :, 0:1]
                if layer == 1:
                    tt(le[:, :, 0:n], lg[:, :, 0:n], largest.to_broadcast([P, NT, n]), ALU.subtract)
                tt(le[:, :, E1:E1 + k], top[:, :, 0:k], largest.to_broadcast([P, NT, k]), ALU.subtract).then_inc(r_le[layer], 1)

            def router_index(layer, b):
                n, k = experts[layer], chosen[layer]
                for t in range(NT):
                    ins = nc.vector.max_index(tix[:, t, :], top[:, t, :], lg[:, t, 0:n])
                link(ins)
                link(nc.vector.tensor_copy(tif[:], tix[:]))

            def router_hot(layer, b):
                n, k = experts[layer], chosen[layer]
                link(tt(hot[:, 0:k, 0:NT * n].rearrange("p k (t e) -> p k t e", e=n),
                        iota[:, 0:n].unsqueeze(1).unsqueeze(1).to_broadcast([P, k, NT, n]),
                        tif[:, :, 0:k].rearrange("p t k -> p k t").unsqueeze(3).to_broadcast([P, k, NT, n]), ALU.is_equal))
                m = NT * n
                if k == 2:
                    tt(mask_h[:, 0:m], hot[:, 0, 0:m], hot[:, 1, 0:m], ALU.add).then_inc(r_mask[layer], 1)
                else:
                    link(tt(pick[:, 0:2, 0:m], hot[:, 0:2, 0:m], hot[:, 2:4, 0:m], ALU.add))
                    tt(mask_h[:, 0:m], pick[:, 0, 0:m], pick[:, 1, 0:m], ALU.add).then_inc(r_mask[layer], 1)

            def router_slots(layer, par):
                n, k = experts[layer], chosen[layer]
                m = NT * n
                dve.wait_ge(r_rank[layer], 1)
                nc.vector.tensor_copy(ranks_sb[:, 0:m + n], ranks_ps[:, 0:m + n]).then_inc(r_read[layer], 1)
                dve.wait_ge(r_read[layer], 1)
                total = ranks_sb[:, m:m + n]
                link(nc.vector.tensor_scalar(tot_i[:, 0:n], total, float(P - 1), None, ALU.add))
                link(nc.vector.tensor_single_scalar(tiles_i[:, 0:n], tot_i[:, 0:n], 7, ALU.logical_shift_right))
                link(nc.vector.tensor_copy(ntile[:, 0:n], tiles_i[:, 0:n]))
                link(nc.vector.tensor_tensor_scan(endt[:, 0:n], ones[:, 0:n], ntile[:, 0:n], 0.0, ALU.mult, ALU.add))
                link(nc.vector.tensor_scalar(below[:, 0:n], endt[:, 0:n], part[:, 0:1], None, ALU.is_le))
                link(nc.vector.tensor_reduce(ecol[:], below[:, 0:n], AX.X, ALU.add))
                nc.vector.tensor_scalar(ecol[:], ecol[:], float(n - 1), None, ALU.min).then_inc(r_col[layer], 1)
                link(tt(base[:, 0:n], endt[:, 0:n], ntile[:, 0:n], ALU.subtract))

            def router_values(layer):
                n, k = experts[layer], chosen[layer]
                m = NT * n
                total = ranks_sb[:, m:m + n]
                rank = ranks_sb[:, 0:m].rearrange("p (t e) -> p t e", e=n)
                tiled = lambda v: v[:, 0:n].unsqueeze(1).to_broadcast([P, NT, n])
                wide = lambda v: v[:, 0:m].rearrange("p (t e) -> p t e", e=n)
                last = nc.vector.scalar_tensor_tensor(wide(val), tiled(base), float(P), rank, ALU.mult, ALU.add)
                if layer == 1:
                    link(tt(wide(seen), rank, tiled(running), ALU.add))
                    link(nc.vector.tensor_scalar(seen, seen, float(CAP), DROP, ALU.is_ge, ALU.mult))
                    link(tt(val[:], val[:], seen, ALU.add))
                    last = tt(running[:], running[:], total, ALU.add)
                link(last)

            def router_pick(layer, par):
                n, k = experts[layer], chosen[layer]
                m = NT * n
                link(tt(pick[:, 0:k, 0:m], hot[:, 0:k, 0:m], val[:, 0:m].unsqueeze(1).to_broadcast([P, k, m]), ALU.mult))
                link(nc.vector.tensor_reduce(slot[:, 0:k * NT].rearrange("p (k t) -> p k t", k=k),
                                             pick[:, 0:k, 0:m].rearrange("p k (t e) -> p k t e", e=n), AX.X, ALU.add))
                if layer == 1:
                    link(nc.vector.tensor_scalar(over[:], slot[:], DROP, None, ALU.is_ge))
                    nc.vector.scalar_tensor_tensor(slots[1 + par][:], over[:], -DROP, slot[:], ALU.mult, ALU.add).then_inc(r_slot[1], 1)
                else:
                    nc.vector.tensor_copy(slots[0][:, 0:k * NT], slot[:, 0:k * NT]).then_inc(r_slot[0], 1)

            def router_weights(layer, par):
                n, k = experts[layer], chosen[layer]
                dve.wait_ge(r_ex[layer], 1)
                among = ex[:, :, E1:E1 + k] if layer == 0 else ex[:, :, 0:n]
                link(nc.vector.tensor_reduce(esum[:], among, AX.X, ALU.add))
                link(nc.vector.reciprocal(rsum[:], esum[:]))
                w = wk[layer * (1 + par)][:, :, 0:k]
                link(tt(w, ex[:, :, E1:E1 + k], rsum[:].unsqueeze(2).to_broadcast([P, NT, k]), ALU.mult))
                if layer == 1:
                    dve.wait_ge(r_slot[1], 1)
                    link(nc.vector.tensor_scalar(over[:], over[:], -1.0, 1.0, ALU.mult, ALU.add))
                    link(tt(w, w, over[:].rearrange("p (k t) -> p t k", k=k), ALU.mult))

            def expert_table(layer):
                dve.wait_ge(r_row[layer], 1)
                nc.vector.tensor_scalar(etab[layer][:], ranks_ps[0:1, 0:n_tiles[layer]], float(D), None,
                                        ALU.mult).then_inc(r_tab[layer], 1)

            def mixture(work, between):
                for i in range(len(work) + 1):
                    if i < len(work):
                        dve.wait_ge(m_sg, i + 1)
                        if i >= 2:
                            dve.wait_ge(m_t, i - 1)
                        ps, f = gate_up_ps(work, i)[1], W[work[i][0]]
                        v = lambda q: q[:, i % 2, 0:GRP * f].rearrange("p (t f) -> p t f", f=f)
                        tt(v(hm), v(sg), ps[:, :, 1, :], ALU.mult).then_inc(m_hm, 1)
                    if i:
                        k = i - 1
                        f = W[work[k][0]]
                        dve.wait_ge(m_t, k + 1)
                        if k >= 2:
                            dve.wait_ge(m_d, k - 1)
                        cols = GRP * f
                        for half in range(P // f):
                            ins = nc.vector.tensor_copy(hT[0:f, k % 2, half * cols:(half + 1) * cols],
                                                        bank[3][half * f:(half + 1) * f, 0:cols])
                        ins.then_inc(m_hT, 1)
                    between(i)

            def sum_tiles(layer, par, tiles, back):
                k = chosen[layer]
                for j in range(k):
                    for t in tiles:
                        if j == 0:
                            dve.wait_ge(e_back[layer][t], back)
                        w = wk[layer * (1 + par)][:, t, j:j + 1]
                        src = yk[:, t % (YK // k) * k + j, :]
                        if j == 0 and layer == 0:
                            ins = nc.vector.tensor_scalar(acc[:, t, :], src, w, None, ALU.mult)
                        else:
                            ins = nc.vector.scalar_tensor_tensor(acc[:, t, :], src, w, z[par][:, t, :] if j == 0 else acc[:, t, :],
                                                                 ALU.mult, ALU.add)
                        if j == k - 1:
                            ins.then_inc(m_sum[layer], 1)
                    if j < k - 1:
                        link(ins)

            def end_block(layer, par, h):
                half = lambda v: v[:, h * HALF:(h + 1) * HALF, :]
                s, dst, ready = (z, x, x1_ready) if layer == 0 else (ret, z, y_ready)
                dve.wait_ge(m_g[layer], h + 1)
                link(tt(half(acc), half(acc), half(s[par]), ALU.mult))
                tt(half(dst[par]), half(acc), half(x[par]), ALU.add).then_inc(ready, 1)
                dve.wait_ge(ready, h + 1)

            def shared():
                for h in range(2):
                    dve.wait_ge(z_s, h + 1)
                    tt(zT[h], zs, bank[3 + 2 * h], ALU.mult).then_inc(z_h, 1)

            def group_norm_1(par, work):
                gdev, gsq = work
                r3 = grp(ret[par][:].rearrange("p t d -> p (t d)"))
                link(nc.vector.tensor_reduce(gsum[:], r3, AX.X, ALU.add))
                link(nc.vector.tensor_scalar(gsum[:], gsum[:], 1.0 / GW, None, ALU.mult))
                link(tt(grp(gdev), r3, one(gsum), ALU.subtract))
                link(tt(gsq, gdev, gdev, ALU.mult))
                link(nc.vector.tensor_reduce(gvar[:], grp(gsq), AX.X, ALU.add))
                nc.vector.tensor_scalar(gvar[:], gvar[:], 1.0 / GW, None, ALU.mult).then_inc(g_var, 1)

            def group_norm_2(par, work):
                gdev, gsq = work
                dve.wait_ge(g_std, 1)
                link(nc.vector.reciprocal(grs[:], gstd[:]))
                link(tt(grp(gdev), grp(gdev), one(grs), ALU.mult))

            def group_norm_3(par, work):
                gdev, gsq = work
                link(tt(ret[par][:], gdev.rearrange("p (t d) -> p t d", d=D), every(gnw), ALU.mult))
                link(tt(ret[par][:], ret[par][:], every(gnb), ALU.add))

            grp = lambda v: v.rearrange("p (g w) -> p g w", w=GW)
            one = lambda v: v[:].unsqueeze(2).to_broadcast([P, NT * GROUPS, GW])
            every = lambda v: v[:].unsqueeze(1).to_broadcast([P, NT, D])

            def chunk_lo(i):
                dve.wait_ge(t_hi, i + 1)
                if i >= 2:
                    dve.wait_ge(t_proj, 6 * (i - 1))
                c = CHUNK(i)
                tt(x_lo[:, i % 2, :], xT[:, c * P:(c + 1) * P], x_hi[:, i % 2, :], ALU.subtract).then_inc(t_lo, 1)

            def rope(i, j):
                c = CHUNK(i)
                dve.wait_ge(t_raw, 4 * i + j + 1)
                x = rp[:, j // 2, (j % 2) * BANK:(j % 2 + 1) * BANK].rearrange("p (h d) -> p h d", h=HB)[:, :, 0:ROPE]
                pairs = lambda v: v.rearrange("p h (i two) -> p h i two", two=2)
                swapped = pairs(x)[:, :, :, ::-1]
                sn = sin[:, c, :].rearrange("p (i two) -> p i two", two=2).unsqueeze(1).to_broadcast([P, HB, ROPE // 2, 2])
                link(tt(pairs(rsn[:]), swapped, sn, ALU.mult))
                link(tt(x, x, cos[:, c, :].unsqueeze(1).to_broadcast([P, HB, ROPE]), ALU.mult))
                tt(x, x, rsn[:], ALU.add).then_inc(t_rope, 1)
                dve.wait_ge(t_rope, 4 * i + j + 1)

            def causal_part(i, h):
                dve.wait_ge(t_a, 2 * i + h + 1)
                if i:
                    dve.wait_ge(t_o, i)
                tt(rA[:, h * BANK:(h + 1) * BANK].rearrange("p (h k) -> p h k", h=HB),
                   bank[product_bank(i, h)].rearrange("p (h k) -> p h k", h=HB),
                   causal[:].unsqueeze(1).to_broadcast([P, HB, P]), ALU.mult).then_inc(t_am, 1)

            def add_state(i, h):
                half = slice(h * BANK, (h + 1) * BANK)
                dve.wait_ge(t_g, 2 * i + h + 1)
                if i == 0:
                    ins = nc.vector.tensor_copy(rS[1][:, half], bank[5 + h])
                else:
                    dve.wait_ge(t_gs, 2 * i)
                    ins = tt(rS[(i + 1) % 2][:, half], rS[i % 2][:, half], bank[5 + h], ALU.add)
                ins.then_inc(t_gs, 1)

            def retained(i, par):
                c = CHUNK(i)
                dve.wait_ge(t_o, i + 1)
                nc.vector.tensor_scalar(ret[par][:, c, :], bank[7][:, 0:D], undecay[:, c:c + 1], None, ALU.mult).then_inc(t_od, 1)

            dve.wait_ge(x_first, 16)
            ln_stats(2, x[0])
            ln_norm(2, x[0])

            def turn(b, par, prev, more):
                if prev:
                    group_norm_1(1 - par, g_beside)
                router_logits(0, b)
                router_choose(0, b)
                router_index(0, b)
                router_hot(0, b)
                for q in range(NT + 2):
                    if q < NT:
                        dve.wait_ge(a_s, q + 1)
                        s_ps = psum[:, (q % 2) * 2 * BANK:(q % 2 + 1) * 2 * BANK]
                        nc.vector.tensor_reduce(nmx[:, q:q + 1], s_ps, AX.X, ALU.max, negate=True).then_inc(a_nmx, 1)
                    if q == 0:
                        for h in range(2):
                            dve.wait_ge(a_proj, 5 + h)
                            nc.vector.tensor_copy(v0[:, h * HALF:(h + 1) * HALF, :].rearrange("p t d -> p (t d)"),
                                                  bank[6 + h]).then_inc(a_v, 1)
                    if 1 <= q <= NT:
                        r = q - 1
                        dve.wait_ge(a_pT, 2 * r + 1)
                        if r >= 2:
                            dve.wait_ge(a_o, r - 1)
                        nc.vector.tensor_copy(pT[r % 2][:, 0:BANK], bank[4]).then_inc(a_pTd, 1)
                        dve.wait_ge(a_p, r + 1)
                        link(nc.vector.reciprocal(rden[:, r:r + 1], den[:, r:r + 1]))
                    if q >= 2:
                        r = q - 2
                        dve.wait_ge(a_o, r + 1)
                        nc.vector.tensor_scalar(z[par][:, r, :], bank[6][:, 0:D], rden[:, r:r + 1], None, ALU.mult).then_inc(a_od, 1)
                    if q == 2:
                        router_slots(0, 0)
                        router_values(0)
                        router_pick(0, 0)
                    if q == 3:
                        expert_table(0)
                        router_weights(0, 0)
                    if q == 4 and prev:
                        group_norm_2(1 - par, g_beside)
                    if q == 6 and prev:
                        group_norm_3(1 - par, g_beside)
                dve.wait_ge(a_od, NT)
                back0 = b * (16 * K0) + 16 * K0
                if prev:
                    def between(i):
                        if i in SUM0:
                            sum_tiles(0, 0, PAIRS[SUM0.index(i)], back0)
                        if i in END0:
                            end_block(0, par, END0.index(i))
                        if i == STATS1[0]:
                            ln_stats_half(x[par], 0)
                        if i == STATS1[1]:
                            ln_stats(1, x[par], first=False)
                        if i == NORM1:
                            ln_norm(1, x[par])
                    mixture(groups_of(0, 1), between)
                else:
                    mixture(groups_of(0), lambda i: None)
                    for tiles in PAIRS:
                        sum_tiles(0, 0, tiles, back0)
                    end_block(0, par, 0)
                    end_block(0, par, 1)
                    ln_stats(1, x[par])
                    ln_norm(1, x[par])

                router_logits(1, b)
                chunk_lo(0)
                chunk_lo(1)
                if not prev:
                    dve.wait_ge(s_w[2], 16 * n_loads[2])
                    for j in range(3):
                        dve.wait_ge(w_hi, j + 1)
                        tt(w1_lo[:, j, :], wqkv1[j], w1_hi[:, j, :], ALU.subtract).then_inc(w_lo, 1)
                shared()
                for j in range(4):
                    rope(0, j)
                for i in range(NT):
                    if i + 2 < NT:
                        chunk_lo(i + 2)
                    for j in range(4):
                        if i + 1 < NT:
                            rope(i + 1, j)
                        if j < 2:
                            causal_part(i, j)
                        elif i + 1 < NT:
                            add_state(i, j - 2)
                        if (i, j) == (0, 0):
                            router_choose(1, b)
                        if (i, j) == (0, 1):
                            router_index(1, b)
                        if (i, j) == (0, 2):
                            router_hot(1, b)
                        if (i, j) == (1, 2):
                            router_slots(1, par)
                        if (i, j) == (1, 3):
                            router_values(1)
                        if (i, j) == (1, 3):
                            router_pick(1, par)
                        if (i, j) == (3, 1):
                            router_weights(1, par)
                        if (i, j) == (2, 1):
                            expert_table(1)
                        if more and (i, j) == STATS0:
                            dve.wait_ge(x_in, 16)
                            ln_stats(0, x[1 - par])
                        if more and (i, j) == NORM0:
                            ln_norm(0, x[1 - par])
                        if prev and (i, j) in SUM1:
                            sum_tiles(1, 1 - par, PAIRS[SUM1.index((i, j))], b * (16 * K1))
                        if prev and (i, j) in END1:
                            end_block(1, 1 - par, END1.index((i, j)))
                    retained(i, par)
                end_turn(dve, b)
                chain.n = 0

            turns(dve, turn)
            group_norm_1((B - 1) % 2, g_behind)
            group_norm_2((B - 1) % 2, g_behind)
            group_norm_3((B - 1) % 2, g_behind)
            mixture(groups_of(1), lambda i: None)
            for h in range(2):
                for tiles in PAIRS[2 * h:2 * h + 2]:
                    sum_tiles(1, (B - 1) % 2, tiles, B * (16 * K1))
                end_block(1, (B - 1) % 2, h)

        @block.tensor
        def _(pe):
            mm, transpose = nc.tensor.matmul, nc.tensor.transpose
            pe.wait_ge(s_w[0], 16 * n_loads[0])
            pe.wait_ge(s_const, 6)

            def columns(z, n, w=P):
                return z[:, n * w:(n + 1) * w]

            def transposed(layer, ln=None):
                for h in range(2):
                    for t in range(HALF):
                        if ln is not None:
                            pe.wait_ge(ln, h * HALF + t + 1)
                        ins = transpose(columns(bank[h], t), xn[layer][:, h * HALF + t, :], ident[:])
                    ins.then_inc(xT_ps[layer], 1)
                pe.wait_ge(xT_sb[layer], 2)

            def router(layer, b):
                n = experts[layer]
                for t in range(NT):
                    ins = mm(columns(bank[7], t, n), columns(xT, t), wr[layer][:], start=True, stop=True)
                ins.then_inc(r_lg[layer], 1)

            def ranks(layer, b):
                n = experts[layer]
                m = NT * n
                pe.wait_ge(r_mask[layer], 1)
                mm(ranks_ps[:, 0:m], before_h[:], mask_h[:, 0:m], start=True, stop=False)
                for j in range(1, NT):
                    mm(ranks_ps[:, j * n:m], ones_h[:], mask_h[:, 0:m - j * n], start=False, stop=j == NT - 1)
                for t in range(NT):
                    ins = mm(ranks_ps[:, m:m + n], ones_h[:], columns(mask_h, t, n), start=t == 0, stop=t == NT - 1)
                ins.then_inc(r_rank[layer], 1)

            def expert_row(layer):
                n = n_tiles[layer]
                pe.wait_ge(r_read[layer], 1)
                pe.wait_ge(r_col[layer], 1)
                mm(ranks_ps[0:1, 0:n], ecol[:], ident[:, 0:n], start=True, stop=True).then_inc(r_row[layer], 1)

            def rows(i):
                pe.wait_ge(e_in[i % XE], 16 * (i // XE + 1))
                if i:
                    pe.wait_ge(m_xT, i)
                for t in range(GRP):
                    ins = transpose(columns(bank[0], t), xe[i % XE][:, t, :], ident[:])
                ins.then_inc(m_x, 1)

            def mixture(work, ahead=0):
                expert = {}

                def read_experts(i):
                    layer, g = work[i]
                    _, expert[i] = nc.values_load_multi_w_load_instructions(
                        etab[layer][0:1, g * GRP:(g + 1) * GRP], engines=[mybir.EngineType.PE], min_val=0,
                        max_val=(experts[layer] - 1) * D,
                        skip_runtime_bounds_check_because="router_slots keeps every tile's expert within the experts")

                def gate_and_up(i):
                    layer, g = work[i]
                    pe.wait_ge(m_xT, i + 1)
                    if i >= 2:
                        pe.wait_ge(m_hm, i - 1)
                    if layer == 0 and i == 1:
                        pe.wait_ge(a_od, NT)
                    f = W[layer]
                    ps = gate_up_ps(work, i)[0]
                    weights = gu[layer][:].rearrange("p e f -> p (e f)")
                    for t in range(GRP):
                        at = expert[i][t] * 2 if layer == 0 else expert[i][t]
                        ins = mm(columns(ps, t, 2 * f), columns(xeT[:, i % 2, :], t), weights[:, bass.ds(at, 2 * f)],
                                 start=True, stop=True)
                    ins.then_inc(m_gu, 1)

                def hidden(i):
                    pe.wait_ge(m_hm, i + 1)
                    if i:
                        pe.wait_ge(m_hT, i)
                    for t in range(GRP * W[work[i][0]] // P):
                        ins = transpose(columns(bank[3], t), columns(hm[:, i % 2, :], t), ident[:])
                    ins.then_inc(m_t, 1)

                def answers(i):
                    layer, g = work[i]
                    f = W[layer]
                    pe.wait_ge(m_hT, i + 1)
                    if i >= 2:
                        pe.wait_ge(m_y, i - 1)
                    weights = dn[layer][:].rearrange("p e d -> p (e d)")
                    for t in range(GRP):
                        per = P // f
                        at = t % per * (GRP // per) + t // per
                        ins = mm(columns(bank[4 + i % 2], t), columns(hT[0:f, i % 2, :], at),
                                 weights[:, bass.ds(expert[i][t], D)], start=True, stop=True)
                    ins.then_inc(m_d, 1)

                read_experts(0)
                for i in range(len(work) + 3):
                    if ahead <= i < len(work):
                        rows(i)
                    if 1 <= i <= len(work):
                        gate_and_up(i - 1)
                    if 2 <= i < len(work) + 2:
                        hidden(i - 2)
                    if i >= 3:
                        answers(i - 3)
                    if i + 1 < len(work):
                        read_experts(i + 1)

            def shared():
                for h in range(2):
                    mm(bank[2 + 2 * h], gus[:, 0, :], columns(xT, h, BANK), start=True, stop=True)
                    mm(bank[3 + 2 * h], gus[:, 1, :], columns(xT, h, BANK), start=True, stop=True).then_inc(z_gu, 1)
                pe.wait_ge(r_ev[1], 1)
                for h in range(2):
                    pe.wait_ge(z_h, h + 1)
                    for t in range(HALF):
                        ins = mm(columns(bank[6 + h], t), columns(zT[h], t), dns[:], start=True, stop=True)
                    ins.then_inc(z_d, 1)

            def turn(b, par, prev, more):
                transposed(0, None if prev else ln_xn[2])
                router(0, b)
                for j in range(4):
                    mm(bank[2 + j], wqkv0[:, j // 2, :], columns(xT, j % 2, BANK), start=True, stop=True).then_inc(a_proj, 1)

                def project_v(h):
                    if h == 1:
                        pe.wait_ge(r_ev[0], 1)
                    for t in range(HALF):
                        ins = mm(columns(bank[6 + h], t), columns(xT, h * HALF + t), wqkv0[:, 2, :], start=True, stop=True)
                    ins.then_inc(a_proj, 1)

                def scores(q):
                    if q == 0:
                        pe.wait_ge(a_qk, 4)
                    if q >= 2:
                        pe.wait_ge(a_p, q - 1)
                    for h in range(2):
                        ins = mm(bank[(q % 2) * 2 + h], columns(qT, q), columns(kT, h, BANK), start=True, stop=True)
                    ins.then_inc(a_s, 1)

                def attend(q):
                    pe.wait_ge(a_pTd, q + 1)
                    pe.wait_ge(a_pTa, q + 1)
                    if q == 1:
                        expert_row(0)
                    if q:
                        pe.wait_ge(a_od, q)
                    for k in range(NT):
                        ins = mm(bank[6][:, 0:D], columns(pT[q % 2], k), v0[:, k, :], start=k == 0, stop=k == NT - 1)
                    ins.then_inc(a_o, 1)

                project_v(0)
                scores(0)
                project_v(1)
                for q in range(NT):
                    if q + 1 < NT:
                        scores(q + 1)
                    pe.wait_ge(a_p, q + 1)
                    if q:
                        pe.wait_ge(a_pTd, q)
                        pe.wait_ge(a_pTa, q)
                    for h in range(2):
                        for k in range(HALF):
                            ins = transpose(columns(bank[4 + h], k), columns(pr[q % 2], h * HALF + k), ident[:])
                        ins.then_inc(a_pT, 1)
                    if q == 0:
                        pe.wait_ge(a_v, 2)
                        ranks(0, b)
                    if q:
                        attend(q - 1)
                rows(0)
                attend(NT - 1)
                pe.wait_ge(r_tab[0], 1)
                if not prev:
                    pe.wait_ge(s_w[1], 16 * n_loads[1])
                mixture(groups_of(0, 1) if prev else groups_of(0), ahead=1)
                transposed(1, ln_xn[1])
                if not prev:
                    pe.wait_ge(s_w[2], 16 * n_loads[2])
                router(1, b)
                shared()

                def project(i, j):
                    n = 6 * i + j
                    if n >= 2:
                        before_j = (j - 2) % 6
                        bi = i if j >= 2 else i - 1
                        if before_j >= 4:
                            pe.wait_ge(t_v, 2 * bi + before_j - 3)
                        else:
                            pe.wait_ge(t_raw, 4 * bi + before_j + 1)
                    if j == 0:
                        pe.wait_ge(t_lo, i + 1)
                    half = slice((j % 2) * BANK, (j % 2 + 1) * BANK)
                    mm(bank[j % 2], x_hi[:, i % 2, :], w1_hi[:, j // 2, half], start=True, stop=False)
                    mm(bank[j % 2], x_hi[:, i % 2, :], w1_lo[:, j // 2, half], start=False, stop=False)
                    mm(bank[j % 2], x_lo[:, i % 2, :], w1_hi[:, j // 2, half], start=False, stop=True).then_inc(t_proj, 1)

                def transpose_half(i, j):
                    q_or_k, h = j % 2, j // 2
                    pe.wait_ge(t_rope, 4 * i + 2 * q_or_k + h + 1)
                    if 4 * i + j >= 2:
                        pe.wait_ge(t_tT, 4 * i + j - 1)
                    for k in range(HB):
                        ins = transpose(columns(bank[2 + q_or_k], k), columns(rp[:, q_or_k, :], h * HB + k), ident[:])
                    ins.then_inc(t_t, 1)

                def products(i, h):
                    pe.wait_ge(t_tT, 4 * i + 2 * h + 2)
                    if product_bank(i, h) == 0:
                        pe.wait_ge(t_v, 2 * i + 1)
                    elif 2 * i + h:
                        pe.wait_ge(t_am, 2 * i + h)
                    for k in range(HB):
                        m = h * HB + k
                        ins = mm(columns(bank[product_bank(i, h)], k), columns(rQT, m), columns(rKT, m), start=True, stop=True)
                    ins.then_inc(t_a, 1)

                def state(i, h):
                    pe.wait_ge(t_q, i + 1)
                    pe.wait_ge(t_vs, i + 1)
                    if i:
                        pe.wait_ge(t_gs, 2 * (i - 1) + h + 1)
                    for k in range(HB):
                        m = h * HB + k
                        ins = mm(columns(bank[5 + h], k), columns(rQ[i % 2], m), columns(rV[i % 2], m), start=True, stop=True)
                    ins.then_inc(t_g, 1)

                def across(i):
                    if i:
                        pe.wait_ge(t_tT, 4 * i + 4)
                        pe.wait_ge(t_gs, 2 * i)
                        pe.wait_ge(t_od, i)
                        if i == 1:
                            pe.wait_ge(r_read[1], 1)
                        if i == 2:
                            pe.wait_ge(r_tab[1], 1)
                    else:
                        pe.wait_ge(r_ev[1], 1)
                        return
                    for m in range(H):
                        mm(bank[7][:, 0:D], columns(rKT, m), columns(rS[i % 2], m), start=m == 0, stop=False)

                def within(i):
                    pe.wait_ge(t_vs, i + 1)
                    pe.wait_ge(t_am, 2 * i + 2)
                    for m in range(H):
                        ins = mm(bank[7][:, 0:D], columns(rA, m), columns(rV[i % 2], m), start=(i == 0 and m == 0), stop=m == H - 1)
                    ins.then_inc(t_o, 1)

                if not prev:
                    pe.wait_ge(w_lo, 3)
                for j in range(6):
                    project(0, j)
                project(1, 0)
                project(1, 1)
                pe.wait_ge(z_y, 2)
                for j in range(4):
                    transpose_half(0, j)
                for i in range(NT):
                    more = i + 1 < NT
                    steps = [lambda: products(i, 0), lambda: products(i, 1),
                             lambda: more and state(i, 0), lambda: more and state(i, 1),
                             lambda: across(i), lambda: within(i)]
                    for j in range(6):
                        steps[j]()
                        if more and j < 4:
                            project(i + 1, j + 2)
                        if (i, j) in ((1, 1), (2, 1)):
                            pe.wait_ge(t_od, i)
                        if (i, j) == (1, 1):
                            ranks(1, b)
                        if (i, j) == (2, 1):
                            expert_row(1)
                    if i + 2 < NT:
                        project(i + 2, 0)
                    if more:
                        transpose_half(i + 1, 0)
                        transpose_half(i + 1, 1)
                    if i + 2 < NT:
                        project(i + 2, 1)
                    if more:
                        transpose_half(i + 1, 2)
                        transpose_half(i + 1, 3)
                end_turn(pe, b)

            turns(pe, turn)
            mixture(groups_of(1))


_INS = ['L0_attn_X', 'L0_attn_W_Q', 'L0_attn_W_K', 'L0_attn_W_V', 'L0_ffn_router_w', 'L0_ffn_router_b',
        'L0_ffn_we_gate', 'L0_ffn_we_up', 'L0_ffn_we_down', 'L1_attn_W_Q', 'L1_attn_W_K', 'L1_attn_W_V',
        'L1_attn_gn_weight', 'L1_attn_gn_bias', 'L1_ffn_Wg', 'L1_ffn_W1', 'L1_ffn_W2', 'L1_ffn_W3',
        'L1_ffn_Ws1', 'L1_ffn_Ws2', 'L1_ffn_Ws3']


def kernel(**inputs):
    import concourse.bacc as _bacc
    from concourse.bass_utils import run_bass_kernel_spmd as _run

    nc = _bacc.Bacc("TRN2", target_bir_lowering=False, num_devices=1)
    arrays = {name: np.ascontiguousarray(inputs[name]) for name in _INS}
    arrays.update(constants())
    aps = {name: nc.dram_tensor(name, v.shape, mybir.dt.from_np(v.dtype), kind="ExternalInput").ap()
           for name, v in arrays.items()}
    out = nc.dram_tensor("out", (B, T, D), F32, kind="ExternalOutput").ap()
    two_layer_block(nc, aps, out)
    return _run(nc, [arrays], core_ids=[0]).results[0]["out"]
```
